# Optimizing a Trainium2 kernel written in Bass

```python
import numpy as np
import jax
import jax.numpy as jnp

def _softmax(x, axis=-1):
    return jax.nn.softmax(x, axis=axis)

def _gelu(x):
    return jax.nn.gelu(x, approximate=True)

def _silu(x):
    return jax.nn.silu(x)

def _sigmoid(x):
    return jax.nn.sigmoid(x)

def _layernorm(x, axis=-1, eps=1e-05):
    m = jnp.mean(x, axis=axis, keepdims=True)
    v = jnp.var(x, axis=axis, keepdims=True)
    return (x - m) / jnp.sqrt(v + eps)

def _scatter_add(tgt, idx, src, axis=0):
    return tgt.at[idx].add(src)

def _segment_sum(src, seg, n):
    return jax.ops.segment_sum(src, seg, n)
kernel_name = 'mk_decoder_preln_d1_seqx_r4_6c532a'

def setup_inputs(seed: int=0):
    np.random.seed(seed)
    _w = jnp.asarray

    def _rec_inputs():
        import jax
        import jax.numpy as jnp
        _rk = jax.random.key(seed)
        x = 0.0001212 + 1 * jax.random.normal(jax.random.fold_in(_rk, 1), (16, 128, 512), jnp.float32)
        _lenS = 128 - jax.random.randint(jax.random.fold_in(_rk, 7), (16,), 0, max(1, 128 // 4) + 1, jnp.int32)
        _lenS2 = 128 - jax.random.randint(jax.random.fold_in(_rk, 8), (16,), 0, max(1, 128 // 4) + 1, jnp.int32)
        _ctx_2048P = jax.random.normal(jax.random.fold_in(_rk, 11), (16, 16, 512), jnp.float32)
        _ctx_2048c = jax.random.dirichlet(jax.random.fold_in(_rk, 511), 0.3 * jnp.ones((16,), jnp.float32), (16, 128))
        _ctx_2048t = jnp.einsum('bsk,bkd->bsd', _ctx_2048c, _ctx_2048P)
        _ctx_2048t = _ctx_2048t * jax.lax.rsqrt(jnp.mean(jnp.square(_ctx_2048t)) + 1e-12) * 0.953939
        ctx_2048 = 0.000173663 + 1.0001 * (_ctx_2048t + 0.3 * jax.random.normal(jax.random.fold_in(_rk, 611), (16, 128, 512), jnp.float32))
        return (x, ctx_2048)
    x, ctx_2048 = _rec_inputs()

    def _L0_attn_setup():
        import jax, jax.numpy as jnp
        import numpy as np
        B, L, D, H = (2, 512, 512, 16)
        HD = D // H

        def rope(x, seq_len, theta=10000.0):
            d = x.shape[-1]
            freqs = 1.0 / theta ** (jnp.arange(0, d, 2, dtype=x.dtype) / d)
            t = jnp.arange(seq_len, dtype=x.dtype)
            f = jnp.outer(t, freqs)
            sin = jnp.repeat(jnp.sin(f), 2, axis=-1)
            cos = jnp.repeat(jnp.cos(f), 2, axis=-1)
            x1, x2 = (x[..., ::2], x[..., 1::2])
            x_rot = jnp.stack([-x2, x1], axis=-1).reshape(x.shape)
            return x * cos + x_rot * sin
        key = jax.random.key(seed)
        k1, k2, k3 = jax.random.split(key, 3)
        x = jax.random.normal(k1, (B, L, D), dtype=jnp.float32)
        w_qkv = jax.random.normal(k2, (D, 3 * D), dtype=jnp.float32) * (1.0 / np.sqrt(D))
        w_proj = jax.random.normal(k3, (D, D), dtype=jnp.float32) * (1.0 / np.sqrt(D))
        return {'x': x, 'w_qkv': w_qkv, 'w_proj': w_proj}
    _L0_attn_all = _L0_attn_setup()
    _L0_attn_in = {k: v for k, v in _L0_attn_all.items() if k in ('w_qkv', 'w_proj')}
    del _L0_attn_all

    def _L0_xattn_setup():
        import jax, jax.numpy as jnp
        import numpy as np
        B_DIM, T_DIM, C_DIM = (16, 256, 512)

        def _wkv(w, u, k, v):
            Bn, Tn, Cn = k.shape
            NEG_INF = jnp.float32(-1e+38)

            def step(carry, kv_t):
                p, q, o = carry
                kt, vt = kv_t
                no = jnp.maximum(o, u + kt)
                A = jnp.exp(o - no)
                E = jnp.exp(u + kt - no)
                y = (A * p + E * vt) / (A * q + E)
                no2 = jnp.maximum(w + o, kt)
                A2 = jnp.exp(w + o - no2)
                E2 = jnp.exp(kt - no2)
                return ((A2 * p + E2 * vt, A2 * q + E2, no2), y)
            init = (jnp.zeros((Bn, Cn), k.dtype), jnp.zeros((Bn, Cn), k.dtype), jnp.full((Bn, Cn), NEG_INF, k.dtype))
            kT = jnp.moveaxis(k, 1, 0)
            vT = jnp.moveaxis(v, 1, 0)
            _, yT = jax.lax.scan(step, init, (kT, vT))
            return jnp.moveaxis(yT, 0, 1)
        key = jax.random.key(seed)
        k1, k2, k3, k4 = jax.random.split(key, 4)
        w = -jnp.exp(jax.random.normal(k1, (C_DIM,), jnp.float32))
        u = jax.random.normal(k2, (C_DIM,), jnp.float32)
        k = jax.random.normal(k3, (B_DIM, T_DIM, C_DIM), jnp.float32)
        v = jax.random.normal(k4, (B_DIM, T_DIM, C_DIM), jnp.float32)
        return {'B': B_DIM, 'T': T_DIM, 'C': C_DIM, 'w': w, 'u': u, 'k': k, 'v': v}
    _L0_xattn_all = _L0_xattn_setup()
    _L0_xattn_in = {k: v for k, v in _L0_xattn_all.items() if k in ('w', 'u')}
    del _L0_xattn_all

    def _L0_ffn_setup():
        import jax, jax.numpy as jnp
        import numpy as np
        TOP_K = 2
        key = jax.random.key(seed)
        ks = jax.random.split(key, 5)
        B, T, D, E, H = (4, 512, 512, 8, 352)
        s = 1.0 / np.sqrt(D)
        sh = 1.0 / np.sqrt(H)
        return {'x': jax.random.normal(ks[0], (B, T, D), dtype=jnp.float32), 'Wg': jax.random.normal(ks[1], (E, D), dtype=jnp.float32) * s, 'W1': jax.random.normal(ks[2], (E, H, D), dtype=jnp.float32) * s, 'W2': jax.random.normal(ks[3], (E, H, D), dtype=jnp.float32) * s, 'W3': jax.random.normal(ks[4], (E, D, H), dtype=jnp.float32) * sh}
    _L0_ffn_all = _L0_ffn_setup()
    _L0_ffn_in = {k: v for k, v in _L0_ffn_all.items() if k in ('Wg', 'W1', 'W2', 'W3')}
    del _L0_ffn_all
    return {'x': x, 'ctx_2048': ctx_2048, 'L0_attn_w_qkv': _L0_attn_in['w_qkv'], 'L0_attn_w_proj': _L0_attn_in['w_proj'], 'L0_xattn_w': _L0_xattn_in['w'], 'L0_xattn_u': _L0_xattn_in['u'], 'L0_ffn_Wg': _L0_ffn_in['Wg'], 'L0_ffn_W1': _L0_ffn_in['W1'], 'L0_ffn_W2': _L0_ffn_in['W2'], 'L0_ffn_W3': _L0_ffn_in['W3']}

def reference(x, ctx_2048, L0_attn_w_qkv, L0_attn_w_proj, L0_xattn_w, L0_xattn_u, L0_ffn_Wg, L0_ffn_W1, L0_ffn_W2, L0_ffn_W3):
    import jax
    import jax.numpy as jnp

    def _L0_attn_ref(x, w_qkv, w_proj):
        import jax, jax.numpy as jnp
        import numpy as np
        B, L, D, H = (2, 512, 512, 16)
        HD = D // H

        def rope(x, seq_len, theta=10000.0):
            d = x.shape[-1]
            freqs = 1.0 / theta ** (jnp.arange(0, d, 2, dtype=x.dtype) / d)
            t = jnp.arange(seq_len, dtype=x.dtype)
            f = jnp.outer(t, freqs)
            sin = jnp.repeat(jnp.sin(f), 2, axis=-1)
            cos = jnp.repeat(jnp.cos(f), 2, axis=-1)
            x1, x2 = (x[..., ::2], x[..., 1::2])
            x_rot = jnp.stack([-x2, x1], axis=-1).reshape(x.shape)
            return x * cos + x_rot * sin
        Bc, Lc, Dc = x.shape
        scale = 1.0 / np.sqrt(HD)
        qkv = (x @ w_qkv).reshape(Bc, Lc, 3, H, HD)
        q, k, v = (qkv[:, :, 0], qkv[:, :, 1], qkv[:, :, 2])
        q = rope(jnp.transpose(q, (0, 2, 1, 3)), Lc)
        k = rope(jnp.transpose(k, (0, 2, 1, 3)), Lc)
        v = jnp.transpose(v, (0, 2, 1, 3))
        att = jnp.einsum('bhqd,bhkd->bhqk', q, k) * scale
        att = jax.nn.softmax(att, axis=-1)
        out = jnp.einsum('bhqk,bhkd->bhqd', att, v)
        out = jnp.transpose(out, (0, 2, 1, 3)).reshape(Bc, Lc, Dc)
        return out @ w_proj

    def _L0_xattn_ref(B, T, C, w, u, k, v):
        import jax, jax.numpy as jnp
        import numpy as np
        B_DIM, T_DIM, C_DIM = (16, 256, 512)

        def _wkv(w, u, k, v):
            Bn, Tn, Cn = k.shape
            NEG_INF = jnp.float32(-1e+38)

            def step(carry, kv_t):
                p, q, o = carry
                kt, vt = kv_t
                no = jnp.maximum(o, u + kt)
                A = jnp.exp(o - no)
                E = jnp.exp(u + kt - no)
                y = (A * p + E * vt) / (A * q + E)
                no2 = jnp.maximum(w + o, kt)
                A2 = jnp.exp(w + o - no2)
                E2 = jnp.exp(kt - no2)
                return ((A2 * p + E2 * vt, A2 * q + E2, no2), y)
            init = (jnp.zeros((Bn, Cn), k.dtype), jnp.zeros((Bn, Cn), k.dtype), jnp.full((Bn, Cn), NEG_INF, k.dtype))
            kT = jnp.moveaxis(k, 1, 0)
            vT = jnp.moveaxis(v, 1, 0)
            _, yT = jax.lax.scan(step, init, (kT, vT))
            return jnp.moveaxis(yT, 0, 1)
        return _wkv(w, u, k, v)

    def _L0_ffn_ref(x, Wg, W1, W2, W3):
        import jax, jax.numpy as jnp
        import numpy as np
        TOP_K = 2
        E = Wg.shape[0]
        scores = jnp.einsum('btd,ed->bte', x, Wg)
        topk_s, topk_i = jax.lax.top_k(scores, TOP_K)
        probs = jax.nn.softmax(topk_s, axis=-1)
        onehot = (topk_i[..., None] == jnp.arange(E)).astype(x.dtype)
        w = jnp.einsum('btk,btke->bte', probs, onehot)
        y = jnp.zeros_like(x)
        for e in range(E):
            h = jax.nn.silu(jnp.einsum('btd,hd->bth', x, W1[e])) * jnp.einsum('btd,hd->bth', x, W2[e])
            y = y + w[..., e:e + 1] * jnp.einsum('bth,dh->btd', h, W3[e])
        return y
    x = x + _L0_attn_ref(_layernorm(x, axis=-1), L0_attn_w_qkv, L0_attn_w_proj)
    x = x + _L0_xattn_ref(16, 128, 512, L0_xattn_w, L0_xattn_u, _layernorm(x, axis=-1), ctx_2048)
    x = x + _L0_ffn_ref(_layernorm(x, axis=-1), L0_ffn_Wg, L0_ffn_W1, L0_ffn_W2, L0_ffn_W3)
    return x

_drawn_inputs = setup_inputs


def setup_inputs(seed=0):
    import zlib

    import numpy as np

    out = dict(_drawn_inputs(seed))
    spreads = {}
    factors = {}
    for name, (base, spread) in spreads.items():
        noise = np.random.default_rng([zlib.crc32(name.encode()), seed]).standard_normal(out[name].shape)
        drawn = base * np.exp(spread * noise) if base else spread * noise
        out[name] = jnp.asarray(drawn.astype(out[name].dtype))
    for name, factor in factors.items():
        out[name] = (out[name] * factor).astype(out[name].dtype)
    return out
```

```python
from contextlib import ExitStack

import concourse.bass as bass
from concourse import mybir

F32 = mybir.dt.float32
F32R = mybir.dt.float32r
U32 = mybir.dt.uint32
I32 = mybir.dt.int32
ALU = mybir.AluOpType
ACT = mybir.ActivationFunctionType
AX_X = mybir.AxisListType.X

P = 128
D = 512
KD = D // P
H = 16
HD = D // H
HB = P // HD
NEG = -1e38
EPS = 1e-5
E = 8
FH = 352
KF = 3
W12 = KD * 2 * FH
WE = W12 + KF * D
NS = 40
SCALE = float(HD) ** -0.5


CONSTS = [("ident", P), ("cos", HD), ("sin", HD), ("iota", P), ("tri", P), ("ones", P), ("mask", P),
          ("thr", 15), ("tok", 32), ("spare", 1)]


def wait_prev(eng, sem, n):
    if isinstance(n, int) and n <= 0:
        return
    eng.wait_ge(sem, n)


def decoder(nc, x, ctxT, w_qkv, w_proj, wkv_wu, wgT, w_moe, consts, x3_dram, out):
    B = x.shape[0] // P
    with ExitStack() as ctx:
        def sb(name, shape, dt=F32):
            return ctx.enter_context(nc.sbuf_tensor(name, shape, dt))

        def ps(name, shape):
            return ctx.enter_context(nc.psum_tensor(name, shape, F32))

        def sem(name):
            return ctx.enter_context(nc.semaphore(name))

        t0 = ps("t0", [P, D])
        vp = ps("vp", [P, D])
        qk_ps = ps("qk_ps", [P, 2, D])
        tp = ps("tp", [P, 2, D])
        so = ps("so", [P, 2, D])

        xres = sb("xres", [P, B, D])
        wbig = sb("wbig", [P, 4 * WE], F32R)
        q3 = KD * 3 * D
        wqkv_hi = wbig[:, 0:q3].rearrange("p (k n) -> p k n", k=KD)
        wqkv_lo = wbig[:, q3:2 * q3].rearrange("p (k n) -> p k n", k=KD)
        wproj_hi = wbig[:, 2 * q3:2 * q3 + KD * D].rearrange("p (k n) -> p k n", k=KD)
        wproj_lo = wbig[:, 2 * q3 + KD * D:2 * q3 + 2 * KD * D].rearrange("p (k n) -> p k n", k=KD)
        wexp = wbig[:].rearrange("p (b s n) -> p b s n", b=2, s=2)
        wraw = sb("wraw", [P, WE])
        cst = sb("cst", [P, consts.shape[1]])
        at = {}
        off = 0
        for name, width in CONSTS:
            at[name] = cst[:, off:off + width]
            off += width
        idm = at["ident"]
        cos_sb, sin_sb = at["cos"], at["sin"]
        wg_sb = sb("wg_sb", [P, KD, E])
        sc_all = sb("sc_all", [P, B, E])
        ids_sb = sb("ids_sb", [P, NS], U32)
        w_sb = sb("w_sb", [P, NS])
        tab = sb("tab", [P, 4, NS], I32)
        nslot = sb("nslot", [P, 1], I32)
        idg = sb("idg", [P, 1], U32)
        ids_out = sb("ids_out", [P, 1], U32)
        holdp = sb("holdp", [P, 3])
        wu_in = sb("wu_in", [P, 2, KD])
        mv1 = sb("mv1", [P, B, 2])
        bst = sb("bst", [P, B, 6])
        ln1 = sb("ln1", [P, B])
        rstd1 = sb("rstd1", [P, B])
        xn = sb("xn", [P, D])
        xnT_hi = sb("xnT_hi", [P, KD, P], F32R)
        xnT_lo = sb("xnT_lo", [P, KD, P], F32R)
        qk = sb("qk", [P, 2, D])
        vext = sb("vext", [P, H, HD + 1])
        qT = sb("qT", [P, KD, P])
        kblk = sb("kblk", [P, KD, HB, P])
        mx = sb("mx", [P, H])
        nb = sb("nb", [P, H])
        rinv = sb("rinv", [P, H])
        o_sb = sb("o_sb", [P, D])
        oT_hi = sb("oT_hi", [P, KD, P], F32R)
        oT_lo = sb("oT_lo", [P, KD, P], F32R)
        mv2 = sb("mv2", [P, 2])
        bst2 = sb("bst2", [P, 6])
        rstd2 = sb("rstd2", [P, 2])
        kn = sb("kn", [P, D])
        kT = sb("kT", [P, D])
        vT = sb("vT", [P, D])
        wtab = sb("wtab", [P, 2, KD, P])
        omax = sb("omax", [P, 1 + D])
        kk = sb("kk", [P, 2, D])
        rot = kk
        pq = sb("pq", [P, 2, 1 + D])
        yT = sb("yT", [P, D])
        mv3 = sb("mv3", [P, 2])
        bst3 = sb("bst3", [P, 6])
        rstd3 = sb("rstd3", [P, 2])
        eps_c = sb("eps_c", [P, 1])
        hold = sb("hold", [P, 1])
        x3n = sb("x3n", [P, D])
        scratch = sb("scratch", [P, 4 * 2048])
        wqkv_raw = scratch[:, 0:KD * 3 * D].rearrange("p (k n) -> p k n", k=KD)
        wproj_raw = scratch[:, KD * 3 * D:].rearrange("p (k n) -> p k n", k=KD)
        prob = scratch[:, 0:2048].rearrange("p (h n) -> p h n", h=H)
        probT = scratch[:, 2048:4096].rearrange("p (h n) -> p h n", h=H)
        relu = scratch[:, 4096:6144].rearrange("p (s n) -> p s n", s=4)
        ez = scratch[:, 6144:8192].rearrange("p (s n) -> p s n", s=4)
        apq = relu[:, 0:2]
        x3T = relu[:, 2]
        hsb = qT[:].rearrange("p k n -> p (k n)")[:, 0:KF * P]
        gsb = kT[:, 0:FH]
        ea = kk

        names = """const_in w_tab_in wg_in stats1 mean1 lnv1 rstd1_ok xn_ok xnT_ps xhi xlo q_ps k_ps v_ps
        rope_a rope_b rope_c qk_ok ropeq_read ropek_read v_ok qT_ps kT_ps qT_ok kb_act kb_dve zero_ok s_ps
        mx_ok nb_ok exp_ok pt_ps pt_act pt_dve pv_ps rinv_ok o_ok oT_ps ohi olo proj_ps x1_ok st2 mv2_ok
        ln2 rs2 kn_ok knT_ps kT_ok vT_in ev_ok tab_ok om_ok kk_ok dm_ok rl_ok ee_ok p_ok q_ok ap_ok
        nd_ok lnd rd_ok y_ok yT_ps x2_ok st3 mv3_ok ln3 rs3 x3_ok x3_out ones_ok wsplit_act wsplit_dve
        out_done wraw_in wlo_ok whi_ok x2_out spare_out x3T_ps x3T_ok sc_ps sc_ok top_ok oh_ok
        ds_ok e12_ok rk_ps sl_ok sel_ok inv_ps tab_set step m_idg m_xg m_xT m_xhi m_xlo m_gu m_silu m_h m_hT
        m_hhi m_hlo m_y m_yok m_sc held held_x held_y""".split()
        s = {n: sem(n) for n in names}
        x_in = [sem(f"x_in{g}") for g in range(4)]
        wq_in = [sem(f"wq_in{k}") for k in range(KD)]
        wp_in = sem("wp_in")

        block = ctx.enter_context(nc.Block())

        def schedule(eng, body):
            for i in range(4):
                body(i, True, i >= 1, i >= 2, i >= 3)
            with eng.Fori(4, B) as i:
                body(i, True, True, True, True)
            for i in range(B, B + 3):
                body(i, False, i < B + 1, i < B + 2, True)

        def slots(eng, body):
            n = eng.value_load(nslot[0:1, 0:1], min_val=E - 3, max_val=NS - 4) + 3
            for k in range(3):
                body(k, True, k >= 1, k >= 2)
            with eng.Fori(3, n) as k:
                body(k, True, True, True)
            body(n, False, True, True)
            body(n + 1, False, False, True)

        def split_next(eng, k, rest):
            starts = eng.value_load(tab[0:1, 2, bass.ds(k - 2, 1)], min_val=0, max_val=1)
            other = eng.value_load(tab[0:1, 3, bass.ds(k - 2, 1)], min_val=0, max_val=1)
            nxt = eng.value_load(tab[0:1, 1, bass.ds(k - 2, 1)], min_val=1, max_val=E)
            with eng.If(starts == 1):
                wait_prev(eng, s["m_y"], k - 2)
                hi = wexp[:, bass.ds(other, 1), 0, :].rearrange("p o n -> p (o n)")
                lo = wexp[:, bass.ds(other, 1), 1, :].rearrange("p o n -> p (o n)")
                if rest:
                    eng.wait_ge(s["whi_ok"], nxt + 1)
                    nc.vector.tensor_tensor(lo, wraw[:], hi.bitcast(F32), ALU.subtract).then_inc(s["wlo_ok"], 1)
                else:
                    eng.wait_ge(s["wraw_in"], 16 * (nxt + 1))
                    nc.scalar.activation(hi, wraw[:], ACT.Copy).then_inc(s["whi_ok"], 1)

        sel_p = wexp[:, 1].rearrange("p s n -> p (s n)")[:, 0:2 * B * P].rearrange("p (a n) -> p a n", n=P)
        sel_v = wexp[:, 1].rearrange("p s n -> p (s n)")[:, 2 * B * P:2 * B * (P + 3 * NS)].rearrange(
            "p (a v n) -> p a v n", v=3, n=NS)
        pos = [0]

        def tmp(*shape):
            n = 1
            for d in shape:
                n *= d
            a = scratch[:, pos[0]:pos[0] + n]
            pos[0] += n
            if len(shape) == 1:
                return a
            names = "abcd"[:len(shape)]
            return a.rearrange(f"p ({' '.join(names)}) -> p {' '.join(names)}", **dict(zip(names, shape)))

        top8, idx8 = tmp(B, 8), tmp(B, 8).bitcast(U32)
        ds12, e12 = tmp(B), tmp(B)
        idxf, oh = tmp(2, B), tmp(2, B, E)
        picked3 = tmp(B, E)
        picked = picked3.rearrange("p b e -> p (b e)")
        vals = tmp(2 * B, 3)

        @block.gpsimd
        def _(pool):
            pool.wait_ge(s["x3_out"], 16 * B)
            pool.wait_ge(s["x2_out"], 16 * B)
            pool.wait_ge(s["spare_out"], 32)
            pool.wait_ge(s["tab_set"], 1)
            nc.gpsimd.memset(holdp[:], 0.0).then_inc(s["held"], 1)
            pool.wait_ge(s["held"], 1)

            def gather():
                nc.gpsimd.indirect_dma_start(xn[:], None, x3_dram, bass.IndirectOffsetOnAxis(ap=idg[:], axis=0)).then_inc(s["m_xg"], 16)

            pool.wait_ge(s["m_idg"], 1)
            gather()

            def carry(c, sem):
                nc.gpsimd.tensor_tensor(holdp[:, c:c + 1], holdp[:, 2:3], holdp[:, 2:3], ALU.add).then_inc(sem, 1)

            def moe(k, X, M1, M2):
                if X:
                    wait_prev(pool, s["held_x"], k)
                    pool.wait_ge(s["m_idg"], k + 2)
                    carry(0, s["held_x"])
                    gather()
                if M2:
                    wait_prev(pool, s["held_y"], k - 2)
                    pool.wait_ge(s["m_yok"], k - 1)
                    carry(1, s["held_y"])
                    nc.gpsimd.indirect_dma_start(out, bass.IndirectOffsetOnAxis(ap=ids_out[:], axis=0), o_sb[:], None,
                                                 compute_op=ALU.add).then_inc(s["m_sc"], 16)
            slots(pool, moe)
            n = pool.value_load(nslot[0:1, 0:1], min_val=E - 3, max_val=NS - 4) + 3
            pool.wait_ge(s["m_sc"], 16 * n)
            pool.wait_ge(s["m_xg"], 16 * (n + 1))

        @block.sync
        def _(sp):
            sp.dma_start(cst[:], consts).then_inc(s["const_in"], 16)
            xv = x.rearrange("(b t) d -> t b d", t=P)
            sp.dma_start(xres[:, 0:B // 4, :], xv[:, 0:B // 4, :]).then_inc(x_in[0], 16)
            for k in range(KD):
                sp.dma_start(wqkv_raw[:, k, :], w_qkv[k * P:(k + 1) * P, :]).then_inc(wq_in[k], 16)
            sp.dma_start(wproj_raw, w_proj.rearrange("(k p) n -> p k n", p=P)).then_inc(wp_in, 16)
            sp.dma_start(wg_sb[:], wgT).then_inc(s["wg_in"], 16)
            sp.dma_start(wu_in[:], wkv_wu).then_inc(s["w_tab_in"], 16)
            for g in range(1, 4):
                a = g * B // 4
                sp.dma_start(xres[:, a:a + B // 4, :], xv[:, a:a + B // 4, :]).then_inc(x_in[g], 16)
            sp.dma_start(wraw[:], w_moe[0]).then_inc(s["wraw_in"], 16)
            sp.wait_ge(s["zero_ok"], 1)
            sp.dma_start(x3_dram[B * P:B * P + P, :], o_sb[:]).then_inc(s["spare_out"], 16)
            sp.dma_start(out[B * P:B * P + P, :], o_sb[:]).then_inc(s["spare_out"], 16)

            def body(i, A, Bs, C, Ds):
                if C:
                    c = i - 2
                    wait_prev(sp, s["ev_ok"], c)
                    sp.dma_start(vT[:].rearrange("p (k t) -> p k t", k=KD), ctxT[bass.ds(c, 1)].rearrange("o p k t -> p (o k) t")).then_inc(s["vT_in"], 16)
                if Ds:
                    e = i - 3
                    sp.wait_ge(s["x2_ok"], e + 1)
                    sp.dma_start(out[bass.ds(e * P, P), :], xres[:, bass.ds(e, 1), :].rearrange("p o n -> p (o n)")).then_inc(s["x2_out"], 16)
                    sp.wait_ge(s["x3_ok"], e + 1)
                    sp.dma_start(x3_dram[bass.ds(e * P, P), :], x3n[:]).then_inc(s["x3_out"], 16)
            schedule(sp, body)
            for e in range(1, E):
                sp.wait_ge(s["wlo_ok"], e)
                sp.dma_start(wraw[:], w_moe[e]).then_inc(s["wraw_in"], 16)
            sp.wait_ge(s["x2_out"], 16 * B)
            sp.wait_ge(s["x3_out"], 16 * B)

        @block.tensor
        def _(pe):
            def three(dst, k, hi, lo, w_hi, w_lo, first, last):
                pe.matmul(dst, hi[:, k, :], w_hi, start=first, stop=False)
                pe.matmul(dst, hi[:, k, :], w_lo, start=False, stop=False)
                return pe.matmul(dst, lo[:, k, :], w_hi, start=False, stop=last)

            def turn(dst, src):
                for k in range(KD):
                    mm = pe.transpose(dst[:, k * P:(k + 1) * P], src[:, k * P:(k + 1) * P], idm)
                return mm

            def project(dst, hi, lo, w_hi, w_lo, a):
                for k in range(KD):
                    mm = three(dst, k, hi, lo, w_hi[:, k, a:a + D], w_lo[:, k, a:a + D], k == 0, k == KD - 1)
                return mm

            pe.wait_ge(s["const_in"], 16)

            def body(i, A, Bs, C, Ds):
                t, c, e = i - 1, i - 2, i - 3

                def score(j):
                    pe.matmul(so[:, j % 2, :], qT[:, j, :], kblk[:, j].rearrange("p r n -> p (r n)"),
                              start=True, stop=True).then_inc(s["s_ps"], 1)

                def turn_prob(j):
                    pe.wait_ge(s["exp_ok"], 4 * t + j + 1)
                    for r in range(HB):
                        mm = pe.transpose(tp[:, j % 2, r * P:(r + 1) * P], prob[:, HB * j + r, :], idm)
                    mm.then_inc(s["pt_ps"], 1)

                def pv(j):
                    for r in range(HB):
                        h = HB * j + r
                        a = (h % 8) * (HD + 1)
                        mm = pe.matmul(so[:, h // 8, a:a + HD + 1], probT[:, h, :], vext[:, h, :], start=True, stop=True)
                    mm.then_inc(s["pv_ps"], 1)

                if Bs:
                    pe.wait_ge(s["qk_ok"], 2 * t + 2)
                    wait_prev(pe, s["olo"], t)
                    turn(tp[:, 0, :], qk[:, 0, :]).then_inc(s["qT_ps"], 1)
                    wait_prev(pe, s["pt_dve"], 2 * t)
                    turn(tp[:, 1, :], qk[:, 1, :]).then_inc(s["kT_ps"], 1)
                if A:
                    pe.wait_ge(s["xn_ok"], i + 1)
                    if isinstance(i, int) and i < 3:
                        wait_prev(pe, s["xlo"], i)
                    elif isinstance(i, int) and i == 3:
                        pe.wait_ge(s["kT_ok"], 1)
                    else:
                        pe.wait_ge(s["sc_ok"], i - 3)
                    turn(t0[:], xn).then_inc(s["xnT_ps"], 1)
                    if isinstance(i, int) and i == 0:
                        pe.wait_ge(s["wsplit_dve"], KD)
                        pe.wait_ge(s["wsplit_act"], KD)
                    pe.wait_ge(s["xhi"], i + 1)
                    pe.wait_ge(s["xlo"], i + 1)
                    wait_prev(pe, s["ropeq_read"], 2 * i)
                    project(qk_ps[:, 0, :], xnT_hi, xnT_lo, wqkv_hi, wqkv_lo, 0).then_inc(s["q_ps"], 1)
                if Bs:
                    pe.wait_ge(s["qT_ok"], t + 1)
                    pe.wait_ge(s["kb_act"], 2 * t + 2)
                    pe.wait_ge(s["kb_dve"], 2 * t + 2)
                    wait_prev(pe, s["o_ok"], 2 * t)
                    score(0)
                    score(1)
                if A:
                    wait_prev(pe, s["ropek_read"], 2 * i)
                    project(qk_ps[:, 1, :], xnT_hi, xnT_lo, wqkv_hi, wqkv_lo, D).then_inc(s["k_ps"], 1)
                if C:
                    pe.wait_ge(s["kn_ok"], c + 1)
                    if not A:
                        pe.wait_ge(s["sc_ok"], i - 3)
                    turn(t0[:], kn).then_inc(s["knT_ps"], 1)
                if Bs:
                    pe.wait_ge(s["exp_ok"], 4 * t + 1)
                    score(2)
                    turn_prob(0)
                    pe.wait_ge(s["exp_ok"], 4 * t + 2)
                    score(3)
                    turn_prob(1)
                if Ds:
                    pe.wait_ge(s["y_ok"], e + 1)
                    if C:
                        pe.wait_ge(s["kT_ok"], c + 1)
                    else:
                        pe.wait_ge(s["sc_ok"], i - 3)
                    turn(t0[:], yT).then_inc(s["yT_ps"], 1)
                if Bs:
                    pe.wait_ge(s["pt_act"], 2 * t + 1)
                    turn_prob(2)
                    pe.wait_ge(s["v_ok"], t + 1)
                    pv(0)
                    pe.wait_ge(s["pt_dve"], 2 * t + 1)
                    pv(1)
                    turn_prob(3)
                    pe.wait_ge(s["pt_act"], 2 * t + 2)
                    pv(2)
                    pe.wait_ge(s["pt_dve"], 2 * t + 2)
                    pv(3)
                if A:
                    if isinstance(i, int) and i < 2:
                        wait_prev(pe, s["v_ok"], i)
                    else:
                        pe.wait_ge(s["x1_ok"], i - 1)
                    project(vp[:], xnT_hi, xnT_lo, wqkv_hi, wqkv_lo, 2 * D).then_inc(s["v_ps"], 1)
                if Bs:
                    pe.wait_ge(s["o_ok"], 2 * t + 2)
                    turn(tp[:, 0, :], o_sb).then_inc(s["oT_ps"], 1)
                if Ds:
                    pe.wait_ge(s["x3_ok"], e + 1)
                    turn(t0[:], x3n).then_inc(s["x3T_ps"], 1)
                if Bs:
                    if A:
                        pe.wait_ge(s["v_ok"], i + 1)
                    else:
                        pe.wait_ge(s["x1_ok"], i - 1)
                    if isinstance(i, int) and i == 1:
                        pe.wait_ge(s["wsplit_dve"], KD + 1)
                        pe.wait_ge(s["wsplit_act"], KD + 1)
                    pe.wait_ge(s["ohi"], t + 1)
                    pe.wait_ge(s["olo"], t + 1)
                    project(vp[:], oT_hi, oT_lo, wproj_hi, wproj_lo, 0).then_inc(s["proj_ps"], 1)
                if Ds:
                    if isinstance(i, int) and i == 3:
                        pe.wait_ge(s["wg_in"], 16)
                    pe.wait_ge(s["x3T_ok"], e + 1)
                    for k in range(KD):
                        mm = pe.matmul(t0[:, 0:E], x3T[:, k * P:(k + 1) * P], wg_sb[:, k, :], start=k == 0, stop=k == KD - 1)
                    mm.then_inc(s["sc_ps"], 1)
            schedule(pe, body)

            pe.wait_ge(s["oh_ok"], 3)
            pe.matmul(t0[:, 0:P], at["tri"], picked, start=True, stop=True)
            pe.matmul(t0[:, P:2 * P], at["ones"], picked, start=True, stop=True).then_inc(s["rk_ps"], 1)
            pe.wait_ge(s["sel_ok"], 2)
            for a in range(2 * B):
                mm = pe.matmul(vp[:, 0:3 * NS], sel_p[:, a, :], sel_v[:, a].rearrange("p v n -> p (v n)"),
                               start=a == 0, stop=a == 2 * B - 1)
            mm.then_inc(s["inv_ps"], 1)

            pe.wait_ge(s["tab_set"], 1)

            def moe(k, X, M1, M2):
                if M2:
                    pe.wait_ge(s["m_h"], k - 1)
                    wait_prev(pe, s["m_hlo"], k - 2)
                    for f in range(KF):
                        n = min(P, FH - f * P)
                        mm = pe.transpose(vp[0:n, f * P:(f + 1) * P], hsb[:, f * P:f * P + n], idm)
                    mm.then_inc(s["m_hT"], 1)
                if X:
                    pe.wait_ge(s["m_xg"], 16 * (k + 1))
                    wait_prev(pe, s["m_xlo"], k)
                    turn(t0[:], xn).then_inc(s["m_xT"], 1)
                if M1:
                    par = pe.value_load(tab[0:1, 0, bass.ds(k - 1, 1)], min_val=0, max_val=1)
                    need = pe.value_load(tab[0:1, 1, bass.ds(k - 1, 1)], min_val=1, max_val=E)
                    pe.wait_ge(s["wlo_ok"], need)
                    pe.wait_ge(s["m_xlo"], k)
                    wait_prev(pe, s["m_h"], k - 1)
                    for g in range(2):
                        for f in range(KD):
                            a = f * 2 * FH + g * FH
                            w_hi = wexp[:, bass.ds(par, 1), 0, a:a + FH].rearrange("p o n -> p (o n)")
                            w_lo = wexp[:, bass.ds(par, 1), 1, a:a + FH].rearrange("p o n -> p (o n)")
                            mm = three(qk_ps[:, g, 0:FH], f, xnT_hi, xnT_lo, w_hi, w_lo, f == 0, f == KD - 1)
                    mm.then_inc(s["m_gu"], 1)
                if M2:
                    par = pe.value_load(tab[0:1, 0, bass.ds(k - 2, 1)], min_val=0, max_val=1)
                    pe.wait_ge(s["m_hlo"], k - 1)
                    wait_prev(pe, s["m_yok"], k - 2)
                    for f in range(KF):
                        n = min(P, FH - f * P)
                        a = W12 + f * D
                        w_hi = wexp[0:n, bass.ds(par, 1), 0, a:a + D].rearrange("p o n -> p (o n)")
                        w_lo = wexp[0:n, bass.ds(par, 1), 1, a:a + D].rearrange("p o n -> p (o n)")
                        mm = three(tp[:, 0, :], f, oT_hi[0:n], oT_lo[0:n], w_hi, w_lo, f == 0, f == KF - 1)
                    mm.then_inc(s["m_y"], 1)
            slots(pe, moe)

        @block.scalar
        def _(act):
            nc.scalar.preload_act_table_set("natural_log_exp_and_others")
            for k in range(KD):
                act.wait_ge(wq_in[k], 16)
                nc.scalar.activation(wqkv_hi[:, k, :], wqkv_raw[:, k, :], ACT.Copy).then_inc(s["wsplit_act"], 1)
            act.wait_ge(wp_in, 16)
            nc.scalar.activation(wproj_hi, wproj_raw, ACT.Copy).then_inc(s["wsplit_act"], 1)
            for g in range(4):
                a, b = g * B // 4, (g + 1) * B // 4
                act.wait_ge(s["mean1"], b)
                nc.scalar.activation(ln1[:, a:b], mv1[:, a:b, 1], ACT.Ln, bias=eps_c[:, 0:1]).then_inc(s["lnv1"], 1)
                act.wait_ge(s["lnv1"], g + 1)
                nc.scalar.activation(rstd1[:, a:b], ln1[:, a:b], ACT.Exp, scale=-0.5).then_inc(s["rstd1_ok"], 1)

            def body(i, A, Bs, C, Ds):
                t, c, e = i - 1, i - 2, i - 3

                def exps(j):
                    act.wait_ge(s["nb_ok"], 4 * t + j + 1)
                    wait_prev(act, s["pt_ps"], 4 * t + j - 3 if not isinstance(t, int) or t > 0 else 0)
                    for r in range(HB):
                        h = HB * j + r
                        a = nc.scalar.activation(prob[:, h, :], so[:, j % 2, r * P:(r + 1) * P], ACT.Exp,
                                                 bias=nb[:, h:h + 1], scale=SCALE)
                    a.then_inc(s["exp_ok"], 1)

                def take_prob(j):
                    act.wait_ge(s["pt_ps"], 4 * t + j + 1)
                    wait_prev(act, s["pv_ps"], 4 * t if not isinstance(t, int) or t > 0 else 0)
                    nc.scalar.activation(probT[:, HB * j:HB * j + HB, :].rearrange("p h n -> p (h n)"),
                                         tp[:, 0, :], ACT.Copy).then_inc(s["pt_act"], 1)

                if A:
                    act.wait_ge(s["xnT_ps"], i + 1)
                    wait_prev(act, s["v_ps"], i)
                    nc.scalar.activation(xnT_hi[:].rearrange("p k n -> p (k n)"), t0[:], ACT.Copy).then_inc(s["xhi"], 1)
                if Bs:
                    act.wait_ge(s["kT_ps"], t + 1)
                    if isinstance(i, int) and i == 1:
                        act.wait_ge(s["zero_ok"], 1)
                    for r in range(2):
                        nc.scalar.activation(kblk[HD * r:HD * r + HD, :, r, :],
                                             tp[HD * r:HD * r + HD, 1, :].rearrange("p (k n) -> p k n", k=KD),
                                             ACT.Copy).then_inc(s["kb_act"], 1)
                    exps(0)
                if C:
                    act.wait_ge(s["knT_ps"], c + 1)
                    wait_prev(act, s["kk_ok"], c)
                    nc.scalar.activation(kT[:], t0[:], ACT.Copy).then_inc(s["kT_ok"], 1)
                if Bs:
                    exps(1)
                    take_prob(0)
                    exps(2)
                    exps(3)
                    take_prob(2)
                if C:
                    act.wait_ge(s["rl_ok"], 2 * c + 2)
                    wait_prev(act, s["nd_ok"], c)
                    nc.scalar.activation(ea[:], relu[:, 0:2, :], ACT.Exp).then_inc(s["ee_ok"], 1)
                    nc.scalar.activation(ez[:].rearrange("p (a b) n -> p a b n", b=2)[:, :, 1, :], relu[:, 2:4, :],
                                         ACT.Exp, scale=-1.0).then_inc(s["ee_ok"], 1)
                if Ds:
                    act.wait_ge(s["mv3_ok"], e + 1)
                    nc.scalar.activation(rstd3[:, 0:1], mv3[:, 1:2], ACT.Ln, bias=eps_c[:, 0:1]).then_inc(s["ln3"], 1)
                    act.wait_ge(s["ln3"], e + 1)
                    nc.scalar.activation(rstd3[:, 1:2], rstd3[:, 0:1], ACT.Exp, scale=-0.5).then_inc(s["rs3"], 1)
                if C:
                    act.wait_ge(s["nd_ok"], c + 1)
                    nc.scalar.activation(kk[:, 0, :], apq[:, 1, :], ACT.Ln).then_inc(s["lnd"], 1)
                    act.wait_ge(s["lnd"], c + 1)
                    nc.scalar.activation(kk[:, 1, :], kk[:, 0, :], ACT.Exp, scale=-1.0).then_inc(s["rd_ok"], 1)
                if A:
                    act.wait_ge(s["v_ps"], i + 1)
                    wait_prev(act, s["pv_ps"], 4 * i)
                    if isinstance(i, int) and i == 0:
                        act.wait_ge(s["zero_ok"], 1)
                    nc.scalar.activation(vext[:, :, 0:HD], vp[:].rearrange("p (h d) -> p h d", h=H),
                                         ACT.Copy).then_inc(s["v_ok"], 1)
                if Bs:
                    act.wait_ge(s["oT_ps"], t + 1)
                    wait_prev(act, s["proj_ps"], t)
                    nc.scalar.activation(oT_hi[:].rearrange("p k n -> p (k n)"), tp[:, 0, :], ACT.Copy).then_inc(s["ohi"], 1)
                if Ds:
                    act.wait_ge(s["x3T_ps"], e + 1)
                    wait_prev(act, s["sc_ps"], e)
                    nc.scalar.activation(x3T, t0[:], ACT.Copy).then_inc(s["x3T_ok"], 1)
                if Bs:
                    act.wait_ge(s["mv2_ok"], t + 1)
                    nc.scalar.activation(rstd2[:, 0:1], mv2[:, 1:2], ACT.Ln, bias=eps_c[:, 0:1]).then_inc(s["ln2"], 1)
                    act.wait_ge(s["ln2"], t + 1)
                    nc.scalar.activation(rstd2[:, 1:2], rstd2[:, 0:1], ACT.Exp, scale=-0.5).then_inc(s["rs2"], 1)
            schedule(act, body)

            act.wait_ge(s["ds_ok"], 1)
            nc.scalar.activation(e12, ds12, ACT.Exp).then_inc(s["e12_ok"], 1)
            act.wait_ge(s["wraw_in"], 16)
            nc.scalar.activation(wexp[:, 0, 0, :], wraw[:], ACT.Copy).then_inc(s["whi_ok"], 1)
            act.wait_ge(s["tab_set"], 1)

            def moe(k, X, M1, M2):
                if M2:
                    split_next(act, k, False)
                    act.wait_ge(s["m_hT"], k - 1)
                    wait_prev(act, s["m_y"], k - 2)
                    nc.scalar.activation(oT_hi[:, 0:KF, :].rearrange("p k n -> p (k n)"), vp[:, 0:KF * P],
                                         ACT.Copy).then_inc(s["m_hhi"], 1)
                if M1:
                    act.wait_ge(s["m_gu"], k)
                    wait_prev(act, s["m_h"], k - 1)
                    nc.scalar.activation(gsb, qk_ps[:, 0, 0:FH], ACT.Silu).then_inc(s["m_silu"], 1)
                if X:
                    act.wait_ge(s["m_xT"], k + 1)
                    wait_prev(act, s["m_gu"], k)
                    nc.scalar.activation(xnT_hi[:].rearrange("p k n -> p (k n)"), t0[:], ACT.Copy).then_inc(s["m_xhi"], 1)
            slots(act, moe)

        @block.vector
        def _(dve):
            v = nc.vector
            v.memset(eps_c[:], EPS)
            for tile in (kblk, omax, pq, o_sb):
                v.memset(tile[:], 0.0)
            v.memset(vext[:, :, HD:HD + 1], 1.0).then_inc(s["zero_ok"], 1)
            dve.wait_ge(s["zero_ok"], 1)
            for g in range(4):
                dve.wait_ge(x_in[g], 16)
                for b in range(g * B // 4, (g + 1) * B // 4):
                    v.bn_stats(bst[:, b, :], xres[:, b, :]).then_inc(s["stats1"], 1)
                    dve.wait_ge(s["stats1"], b + 1)
                    v.bn_aggr(mv1[:, b, :], bst[:, b, :]).then_inc(s["mean1"], 1)
                if g == 0:
                    for k in range(KD):
                        dve.wait_ge(s["wsplit_act"], k + 1)
                        v.tensor_tensor(wqkv_lo[:, k, :], wqkv_raw[:, k, :], wqkv_hi[:, k, :].bitcast(F32),
                                        ALU.subtract).then_inc(s["wsplit_dve"], 1)
                    dve.wait_ge(s["wsplit_act"], KD + 1)
                    v.tensor_tensor(wproj_lo, wproj_raw, wproj_hi.bitcast(F32),
                                    ALU.subtract).then_inc(s["wsplit_dve"], 1)
            dve.wait_ge(s["w_tab_in"], 16)
            v.tensor_copy(wtab[:, 0], wu_in[:, 0, :].rearrange("p (k o) -> p k o", o=1).broadcast_to([P, KD, P])).then_inc(s["tab_ok"], 1)
            v.tensor_scalar(wtab[:, 1], wu_in[:, 1, :].rearrange("p (k o) -> p k o", o=1).broadcast_to([P, KD, P]),
                            -1.0, None, ALU.mult).then_inc(s["tab_ok"], 1)
            dve.wait_ge(s["tab_ok"], 2)
            v.memset(wtab[:, :, :, 0:1], NEG).then_inc(s["tab_ok"], 1)
            dve.wait_ge(s["tab_ok"], 3)
            dve.wait_ge(s["const_in"], 16)

            def normalise(dst, src, mean, rstd):
                return v.tensor_scalar(dst, src, mean, rstd, ALU.subtract, ALU.mult)

            def body(i, A, Bs, C, Ds):
                t, c, e = i - 1, i - 2, i - 3

                def maxes(j):
                    dve.wait_ge(s["s_ps"], 4 * t + j + 1)
                    v.tensor_reduce(mx[:, HB * j:HB * j + HB], so[:, j % 2, :].rearrange("p (r n) -> p r n", r=HB),
                                    AX_X, ALU.max).then_inc(s["mx_ok"], 1)
                    dve.wait_ge(s["mx_ok"], 4 * t + j + 1)
                    v.tensor_scalar(nb[:, HB * j:HB * j + HB], mx[:, HB * j:HB * j + HB], -SCALE, None,
                                    ALU.mult).then_inc(s["nb_ok"], 1)

                def rope(w, ready, read):
                    dve.wait_ge(s[ready], i + 1)
                    src = qk_ps[:, w, :].rearrange("p (h d) -> p h d", h=H)
                    cosb = cos_sb.rearrange("p (o d) -> p o d", o=1).broadcast_to([P, H, HD])
                    v.tensor_tensor(rot[:, w, :].rearrange("p (h d) -> p h d", h=H), src, cosb,
                                    ALU.mult).then_inc(s["rope_a"], 1)
                    s4 = qk_ps[:, w, :].rearrange("p (h d two) -> p h d two", h=H, two=2)
                    d4 = qk[:, w, :].rearrange("p (h d two) -> p h d two", h=H, two=2)
                    for a in range(2):
                        sn = sin_sb.rearrange("p (o d two) -> p o d two", o=1, two=2)[:, :, :, a].broadcast_to([P, H, HD // 2])
                        v.tensor_tensor(d4[:, :, :, a], s4[:, :, :, 1 - a], sn, ALU.mult).then_inc(s[read], 1)
                    dve.wait_ge(s["rope_a"], 2 * i + w + 1)
                    dve.wait_ge(s[read], 2 * i + 2)
                    v.tensor_tensor(qk[:, w, :], qk[:, w, :], rot[:, w, :], ALU.add).then_inc(s["qk_ok"], 1)

                def take_prob(j):
                    dve.wait_ge(s["pt_ps"], 4 * t + j + 1)
                    v.tensor_copy(probT[:, HB * j:HB * j + HB, :].rearrange("p h n -> p (h n)"),
                                  tp[:, 1, :]).then_inc(s["pt_dve"], 1)

                if A:
                    if isinstance(i, int) and i % (B // 4) == 0:
                        dve.wait_ge(s["rstd1_ok"], 4 if i else 1)
                    elif not isinstance(i, int):
                        dve.wait_ge(s["rstd1_ok"], 4)
                    wait_prev(dve, s["xnT_ps"], i)
                    normalise(xn[:], xres[:, bass.ds(i, 1), :].rearrange("p o n -> p (o n)"), mv1[:, bass.ds(i, 1), 0], rstd1[:, bass.ds(i, 1)]).then_inc(s["xn_ok"], 1)
                if Bs:
                    dve.wait_ge(s["qT_ps"], t + 1)
                    v.tensor_copy(qT[:].rearrange("p k n -> p (k n)"), tp[:, 0, :]).then_inc(s["qT_ok"], 1)
                    dve.wait_ge(s["kT_ps"], t + 1)
                    for r in range(2, HB):
                        v.tensor_copy(kblk[HD * r:HD * r + HD, :, r, :],
                                      tp[HD * r:HD * r + HD, 1, :].rearrange("p (k n) -> p k n", k=KD)).then_inc(s["kb_dve"], 1)
                if A:
                    dve.wait_ge(s["xhi"], i + 1)
                    wait_prev(dve, s["v_ps"], i)
                    v.tensor_tensor(xnT_lo[:].rearrange("p k n -> p (k n)"), t0[:],
                                    xnT_hi[:].rearrange("p k n -> p (k n)").bitcast(F32), ALU.subtract).then_inc(s["xlo"], 1)
                if Bs:
                    maxes(0)
                    maxes(1)
                if A:
                    rope(0, "q_ps", "ropeq_read")
                if Bs:
                    maxes(2)
                if A:
                    rope(1, "k_ps", "ropek_read")
                if Bs:
                    maxes(3)
                if C:
                    dve.wait_ge(s["kT_ok"], c + 1)
                    v.tensor_tensor_scan(omax[:, 1:], wtab[:, 0].rearrange("p k n -> p (k n)"), kT[:], 0.0, ALU.add, ALU.max).then_inc(s["om_ok"], 1)
                    v.tensor_tensor(kk[:], kT[:].rearrange("p (o n) -> p o n", o=1).broadcast_to([P, 2, D]),
                                    wtab[:].rearrange("p a k n -> p a (k n)"), ALU.subtract).then_inc(s["kk_ok"], 1)
                    dve.wait_ge(s["om_ok"], c + 1)
                    dve.wait_ge(s["kk_ok"], c + 1)
                    v.tensor_tensor(kk[:], omax[:, 0:D].rearrange("p (o n) -> p o n", o=1).broadcast_to([P, 2, D]),
                                    kk[:], ALU.subtract).then_inc(s["dm_ok"], 1)
                    dve.wait_ge(s["dm_ok"], c + 1)
                    v.tensor_scalar(relu[:, 0:2, :], kk[:], 0.0, None, ALU.min).then_inc(s["rl_ok"], 1)
                    v.tensor_scalar(relu[:, 2:4, :], kk[:], 0.0, None, ALU.max).then_inc(s["rl_ok"], 1)
                if Bs:
                    take_prob(1)
                    take_prob(3)
                if Ds:
                    xr = xres[:, bass.ds(e, 1), :].rearrange("p o n -> p (o n)")
                    dve.wait_ge(s["yT_ps"], e + 1)
                    v.tensor_tensor(xr, xr, t0[:], ALU.add).then_inc(s["x2_ok"], 1)
                    dve.wait_ge(s["x2_ok"], e + 1)
                    v.memset(hold[:], 0.0)
                    v.bn_stats(bst3[:], xr).then_inc(s["st3"], 1)
                    dve.wait_ge(s["st3"], e + 1)
                    v.memset(hold[:], 0.0)
                    v.bn_aggr(mv3[:], bst3[:]).then_inc(s["mv3_ok"], 1)
                if C:
                    ez4 = ez[:].rearrange("p (a b) n -> p a b n", b=2)
                    dve.wait_ge(s["ee_ok"], 2 * c + 2)
                    dve.wait_ge(s["vT_in"], 16 * (c + 1))
                    v.tensor_tensor(ez4[:, :, 0, :], ez4[:, :, 1, :],
                                    vT[:].rearrange("p (o n) -> p o n", o=1).broadcast_to([P, 2, D]), ALU.mult).then_inc(s["ev_ok"], 1)
                    v.tensor_tensor_scan(pq[:, 1, 1:], ea[:, 0, :], ez[:, 1, :], 0.0, ALU.mult, ALU.add).then_inc(s["q_ok"], 1)
                    dve.wait_ge(s["ev_ok"], c + 1)
                    v.tensor_tensor_scan(pq[:, 0, 1:], ea[:, 0, :], ez[:, 0, :], 0.0, ALU.mult, ALU.add).then_inc(s["p_ok"], 1)
                    dve.wait_ge(s["p_ok"], c + 1)
                    dve.wait_ge(s["q_ok"], c + 1)
                    v.tensor_tensor(apq, pq[:, :, 0:D], ea[:, 1, :].rearrange("p (o n) -> p o n", o=1).broadcast_to([P, 2, D]),
                                    ALU.mult).then_inc(s["ap_ok"], 1)
                    dve.wait_ge(s["ap_ok"], c + 1)
                    v.tensor_tensor(apq, apq, ez[:, 2:4, :], ALU.add).then_inc(s["nd_ok"], 1)
                if Bs:
                    for half in range(2):
                        dve.wait_ge(s["pv_ps"], 4 * t + 2 * half + 2)
                        ov = so[:, half, 0:8 * (HD + 1)].rearrange("p (h d) -> p h d", h=8)
                        v.reciprocal(rinv[:, 8 * half:8 * half + 8], ov[:, :, HD]).then_inc(s["rinv_ok"], 1)
                        dve.wait_ge(s["rinv_ok"], 2 * t + half + 1)
                        wait_prev(dve, s["oT_ps"], t)
                        if isinstance(i, int) and i == 1:
                            dve.wait_ge(s["spare_out"], 32)
                        v.tensor_tensor(o_sb[:, half * D // 2:(half + 1) * D // 2].rearrange("p (h d) -> p h d", h=8),
                                        ov[:, :, 0:HD],
                                        rinv[:, 8 * half:8 * half + 8].rearrange("p (h o) -> p h o", o=1).broadcast_to([P, 8, HD]),
                                        ALU.mult).then_inc(s["o_ok"], 1)
                    dve.wait_ge(s["ohi"], t + 1)
                    v.tensor_tensor(oT_lo[:].rearrange("p k n -> p (k n)"), tp[:, 0, :],
                                    oT_hi[:].rearrange("p k n -> p (k n)").bitcast(F32), ALU.subtract).then_inc(s["olo"], 1)
                if Ds:
                    dve.wait_ge(s["rs3"], e + 1)
                    wait_prev(dve, s["x3_out"], 16 * e)
                    normalise(x3n[:], xres[:, bass.ds(e, 1), :].rearrange("p o n -> p (o n)"), mv3[:, 0:1], rstd3[:, 1:2]).then_inc(s["x3_ok"], 1)
                if C:
                    dve.wait_ge(s["rd_ok"], c + 1)
                    wait_prev(dve, s["yT_ps"], c)
                    v.tensor_tensor(yT[:], apq[:, 0, :], kk[:, 1, :], ALU.mult).then_inc(s["y_ok"], 1)
                if Bs:
                    xr = xres[:, bass.ds(t, 1), :].rearrange("p o n -> p (o n)")
                    dve.wait_ge(s["proj_ps"], t + 1)
                    v.tensor_tensor(xr, xr, vp[:], ALU.add).then_inc(s["x1_ok"], 1)
                    dve.wait_ge(s["x1_ok"], t + 1)
                    v.memset(hold[:], 0.0)
                    v.bn_stats(bst2[:], xr).then_inc(s["st2"], 1)
                    dve.wait_ge(s["st2"], t + 1)
                    v.memset(hold[:], 0.0)
                    v.bn_aggr(mv2[:], bst2[:]).then_inc(s["mv2_ok"], 1)
                    dve.wait_ge(s["rs2"], t + 1)
                    wait_prev(dve, s["knT_ps"], t)
                    normalise(kn[:], xr, mv2[:, 0:1], rstd2[:, 1:2]).then_inc(s["kn_ok"], 1)
                if Ds:
                    dve.wait_ge(s["sc_ps"], e + 1)
                    v.tensor_scalar(sc_all[:, bass.ds(e, 1), :].rearrange("p o n -> p (o n)"), t0[:, 0:E], 0.0, None,
                                    ALU.add).then_inc(s["sc_ok"], 1)
            schedule(dve, body)

            nstep = [0]

            def then(ins):
                nstep[0] += 1
                ins.then_inc(s["step"], 1)
                dve.wait_ge(s["step"], nstep[0])

            dve.wait_ge(s["sc_ok"], B)
            for b in range(B):
                v.max(top8[:, b, :], sc_all[:, b, :]).then_inc(s["top_ok"], 1)
            for b in range(B):
                dve.wait_ge(s["top_ok"], b + 1)
                v.max_index(idx8[:, b, :], top8[:, b, :], sc_all[:, b, :]).then_inc(s["step"], 1)
            nstep[0] += B
            dve.wait_ge(s["top_ok"], B)
            v.tensor_tensor(ds12, top8[:, :, 1], top8[:, :, 0], ALU.subtract).then_inc(s["ds_ok"], 1)
            dve.wait_ge(s["step"], nstep[0])
            then(v.tensor_copy(idxf, idx8[:, :, 0:2].rearrange("p b k -> p k b")))
            expert = at["iota"][:, 0:E].rearrange("p (o e) -> p o e", o=1)
            dve.wait_ge(s["const_in"], 16)
            for a in range(2):
                v.tensor_tensor(oh[:, a], expert.broadcast_to([P, B, E]),
                                idxf[:, a].rearrange("p (b o) -> p b o", o=1).broadcast_to([P, B, E]), ALU.is_equal).then_inc(s["oh_ok"], 1)
            dve.wait_ge(s["oh_ok"], 2)
            v.tensor_tensor(picked3, oh[:, 0], oh[:, 1], ALU.add).then_inc(s["oh_ok"], 1)
            dve.wait_ge(s["e12_ok"], 1)
            den, pk = tmp(B), tmp(2, B)
            then(v.tensor_scalar(den, e12, 1.0, None, ALU.add))
            then(v.reciprocal(pk[:, 0], den))
            then(v.tensor_tensor(pk[:, 1], pk[:, 0], e12, ALU.mult))
            phi = sb("phi", [P, 2 * B], F32R)
            pkf = pk.rearrange("p k b -> p (k b)")
            v.tensor_copy(vals[:, :, 0], at["tok"])
            then(v.tensor_copy(phi[:], pkf))
            v.tensor_copy(vals[:, :, 1], phi[:].bitcast(F32))
            then(v.tensor_tensor(vals[:, :, 2], pkf, phi[:].bitcast(F32), ALU.subtract))
            dve.wait_ge(s["rk_ps"], 1)
            tot, cum, cmp, cnt, last, first = tmp(E, B), tmp(E, B), tmp(E, B - 1), tmp(E), tmp(E), tmp(E)
            then(v.tensor_copy(tot, t0[:, P:2 * P].rearrange("p (b e) -> p e b", e=E)))
            then(v.tensor_tensor_scan(cum.rearrange("p e b -> p (e b)"), at["mask"], tot.rearrange("p e b -> p (e b)"),
                                      0.0, ALU.mult, ALU.add))
            then(v.tensor_tensor(cmp, cum[:, :, B - 1:B].broadcast_to([P, E, B - 1]),
                                 at["thr"].rearrange("p (o n) -> p o n", o=1).broadcast_to([P, E, B - 1]), ALU.is_gt))
            then(v.tensor_reduce(cnt, cmp, AX_X, ALU.add))
            then(v.tensor_scalar(cnt, cnt, 1.0, None, ALU.add))
            then(v.tensor_tensor_scan(last, at["ones"][:, 0:E], cnt, 0.0, ALU.mult, ALU.add))
            then(v.tensor_tensor(first, last, cnt, ALU.subtract))
            then(v.tensor_tensor(cum, cum, tot, ALU.subtract))
            then(v.tensor_scalar(first, first, float(P), None, ALU.mult))
            then(v.tensor_tensor(cum, cum, first.rearrange("p (e o) -> p e o", o=1).broadcast_to([P, E, B]), ALU.add))
            sl, pr, row = tmp(B, E), tmp(2, B * E), tmp(2 * B)
            then(v.tensor_tensor(sl, t0[:, 0:P].rearrange("p (b e) -> p b e", e=E), cum.rearrange("p e b -> p b e"), ALU.add))
            then(v.tensor_tensor(pr, oh.rearrange("p a b e -> p a (b e)"),
                                 sl.rearrange("p b e -> p (b e)").rearrange("p (o n) -> p o n", o=1).broadcast_to([P, 2, B * E]), ALU.mult))
            then(v.tensor_reduce(row, pr.rearrange("p a (b e) -> p (a b) e", e=E), AX_X, ALU.add))
            rowi = tmp(2 * B).bitcast(I32)
            divi, modi = tmp(2 * B).bitcast(I32), tmp(2 * B).bitcast(I32)
            divf, modf = tmp(2 * B), tmp(2 * B)
            then(v.tensor_copy(rowi, row))
            v.tensor_scalar(divi, rowi, 7, None, ALU.logical_shift_right)
            then(v.tensor_scalar(modi, rowi, P - 1, None, ALU.bitwise_and))
            v.tensor_copy(divf, divi)
            then(v.tensor_copy(modf, modi))
            one_s = tmp(2 * B, NS)
            then(v.tensor_tensor(one_s, at["iota"][:, 0:NS].rearrange("p (o n) -> p o n", o=1).broadcast_to([P, 2 * B, NS]),
                                 divf.rearrange("p (a o) -> p a o", o=1).broadcast_to([P, 2 * B, NS]), ALU.is_equal))
            v.tensor_tensor(sel_p, at["iota"].rearrange("p (o n) -> p o n", o=1).broadcast_to([P, 2 * B, P]),
                            modf.rearrange("p (a o) -> p a o", o=1).broadcast_to([P, 2 * B, P]), ALU.is_equal).then_inc(s["sel_ok"], 1)
            for w in range(3):
                ins = v.tensor_tensor(sel_v[:, :, w, :], one_s, vals[:, :, w:w + 1].broadcast_to([P, 2 * B, NS]), ALU.mult)
            ins.then_inc(s["sel_ok"], 1)
            sc, es, prev = tmp(NS, E), tmp(NS), tmp(NS)
            then(v.tensor_tensor(sc, at["iota"][:, 0:NS].rearrange("p (n o) -> p n o", o=1).broadcast_to([P, NS, E]),
                                 last.rearrange("p (o e) -> p o e", o=1).broadcast_to([P, NS, E]), ALU.is_ge))
            then(v.tensor_reduce(es, sc, AX_X, ALU.add))
            esi = tmp(NS).bitcast(I32)
            v.tensor_copy(esi, es)
            v.memset(prev[:, 0:1], 1.0)
            then(v.tensor_tensor(prev[:, 1:NS], es[:, 1:NS], es[:, 0:NS - 1], ALU.subtract))
            flag = tmp(NS)
            then(v.tensor_scalar(flag, es, E - 1.0, None, ALU.is_lt))
            then(v.tensor_tensor(flag, flag, prev, ALU.mult))
            v.tensor_scalar(tab[:, 0, :], esi, 1, None, ALU.bitwise_and)
            v.tensor_scalar(tab[:, 1, :], es, 1.0, None, ALU.add)
            v.tensor_copy(tab[:, 2, :], flag)
            v.tensor_scalar(nslot[:, 0:1], last[:, E - 1:E], -3.0, None, ALU.add)
            par = tmp(NS)
            then(v.memset(hold[:], 0.0))
            then(v.tensor_copy(par, tab[:, 0, :]))
            then(v.tensor_scalar(tab[:, 3, :], par, -1.0, 1.0, ALU.mult, ALU.add))
            dve.wait_ge(s["whi_ok"], 1)
            v.tensor_tensor(wexp[:, 0, 1, :], wraw[:], wexp[:, 0, 0, :].bitcast(F32), ALU.subtract).then_inc(s["wlo_ok"], 1)
            dve.wait_ge(s["inv_ps"], 1)
            inv, pad = tmp(3, NS), tmp(NS)
            then(v.tensor_copy(inv, vp[:, 0:3 * NS].rearrange("p (v n) -> p v n", v=3)))
            v.tensor_tensor(w_sb[:], inv[:, 1], inv[:, 2], ALU.add)
            then(v.tensor_scalar(pad, inv[:, 0], 0.0, at["spare"], ALU.is_equal, ALU.mult))
            then(v.scalar_tensor_tensor(out=ids_sb[:], in0=inv[:, 0], scalar=-1.0, in1=pad, op0=ALU.add, op1=ALU.add))
            v.tensor_copy(idg[:], ids_sb[:, 0:1]).then_inc(s["m_idg"], 1)
            v.memset(hold[:], 0.0).then_inc(s["tab_set"], 1)
            dve.wait_ge(s["tab_set"], 1)

            def moe(k, X, M1, M2):
                if M2:
                    split_next(dve, k, True)
                    dve.wait_ge(s["m_hhi"], k - 1)
                    v.tensor_tensor(oT_lo[:, 0:KF, :].rearrange("p k n -> p (k n)"), vp[:, 0:KF * P],
                                    oT_hi[:, 0:KF, :].rearrange("p k n -> p (k n)").bitcast(F32), ALU.subtract).then_inc(s["m_hlo"], 1)
                if M1:
                    dve.wait_ge(s["m_silu"], k)
                    wait_prev(dve, s["m_hT"], k - 1)
                    v.tensor_tensor(hsb[:, 0:FH], qk_ps[:, 1, 0:FH], gsb, ALU.mult).then_inc(s["m_h"], 1)
                if X:
                    dve.wait_ge(s["m_xhi"], k + 1)
                    v.tensor_tensor(xnT_lo[:].rearrange("p k n -> p (k n)"), t0[:],
                                    xnT_hi[:].rearrange("p k n -> p (k n)").bitcast(F32), ALU.subtract).then_inc(s["m_xlo"], 1)
                    v.tensor_scalar(idg[:], ids_sb[:, bass.ds(k + 1, 1)], 0.0, None, ALU.add).then_inc(s["m_idg"], 1)
                if M2:
                    dve.wait_ge(s["m_y"], k - 1)
                    wait_prev(dve, s["m_sc"], 16 * (k - 2))
                    v.tensor_scalar(ids_out[:], ids_sb[:, bass.ds(k - 2, 1)], 0.0, None, ALU.add)
                    v.tensor_scalar(o_sb[:], tp[:, 0, :], w_sb[:, bass.ds(k - 2, 1)], None, ALU.mult).then_inc(s["m_yok"], 1)
            slots(dve, moe)


def kernel(**inputs):
    import numpy as np
    import concourse.bacc as bacc
    from concourse.bass_utils import run_bass_kernel_spmd

    f32 = np.float32
    T, DM, HW = 128, 512, 32
    a = {n: np.ascontiguousarray(v) for n, v in inputs.items()}
    NB = a["x"].shape[0]
    freqs = (1.0 / f32(10000.0) ** (np.arange(0, HW, 2, dtype=f32) / f32(HW))).astype(f32)
    angle = np.outer(np.arange(T, dtype=f32), freqs).astype(f32)
    sin = np.repeat(np.sin(angle), 2, axis=-1)
    sin[:, 0::2] *= -1
    NE, FF, KB = a["L0_ffn_W1"].shape[0], a["L0_ffn_W1"].shape[1], DM // 128
    moe = np.zeros((NE, 128, 2 * KB * FF + 3 * DM), f32)
    w12 = moe[:, :, :2 * KB * FF].reshape(NE, 128, KB, 2, FF)
    for g, n in enumerate(("L0_ffn_W1", "L0_ffn_W2")):
        w12[:, :, :, g, :] = a[n].reshape(NE, FF, KB, 128).transpose(0, 3, 2, 1)
    w3 = moe[:, :, 2 * KB * FF:].reshape(NE, 128, 3, DM)
    for k in range(3):
        n = min(128, FF - 128 * k)
        w3[:, :n, k, :] = a["L0_ffn_W3"][:, :, 128 * k:128 * k + n].transpose(0, 2, 1)
    row = np.arange(128)
    col = lambda v: np.broadcast_to(np.asarray(v, f32), (128, len(v)))
    consts = {
        "ident": np.eye(128), "cos": np.repeat(np.cos(angle), 2, axis=-1), "sin": sin, "iota": col(row),
        "tri": np.triu(np.ones((128, 128)), 1), "ones": np.ones((128, 128)),
        "mask": col(np.tile(np.arange(NB) > 0, NE)), "thr": col(128 * np.arange(1, NB)),
        "tok": row[:, None] + 1 + 128 * np.tile(np.arange(NB), 2)[None, :], "spare": NB * T + 1 + row[:, None],
    }
    arrays = {
        "x": a["x"].reshape(NB * T, DM),
        "ctxT": np.ascontiguousarray(a["ctx_2048"].reshape(NB, T, KB, 128).transpose(0, 3, 2, 1)),
        "w_qkv": a["L0_attn_w_qkv"], "w_proj": a["L0_attn_w_proj"],
        "wkv_wu": np.ascontiguousarray(np.stack([a["L0_xattn_w"], a["L0_xattn_u"]]).reshape(2, KB, 128).transpose(2, 0, 1)),
        "wgT": np.ascontiguousarray(a["L0_ffn_Wg"].reshape(NE, KB, 128).transpose(2, 1, 0)),
        "w_moe": moe,
        "consts": np.concatenate([consts[n].astype(f32) for n, _ in CONSTS], axis=1),
    }
    nc = bacc.Bacc("TRN2", target_bir_lowering=False, num_devices=1)
    args = [nc.dram_tensor(n, v.shape, mybir.dt.from_np(v.dtype), kind="ExternalInput").ap() for n, v in arrays.items()]
    x3 = nc.dram_tensor("x3n_rows", (NB * T + 128, DM), F32).ap()
    out = nc.dram_tensor("y_out", (NB * T + 128, DM), F32, kind="ExternalOutput").ap()
    decoder(nc, *args, x3, out)
    r = run_bass_kernel_spmd(nc, [arrays], core_ids=[0])
    return r.results[0]["y_out"][:NB * T].reshape(NB, T, DM)
```

```python
from contextlib import ExitStack

import concourse.bass as bass
from concourse import mybir

F32 = mybir.dt.float32
F32R = mybir.dt.float32r
U32 = mybir.dt.uint32
I32 = mybir.dt.int32
ALU = mybir.AluOpType
ACT = mybir.ActivationFunctionType
AX_X = mybir.AxisListType.X

P = 128
D = 512
KD = D // P
H = 16
HD = D // H
HB = P // HD
NEG = -1e38
EPS = 1e-5
E = 8
FH = 352
KF = 3
W12 = KD * 2 * FH
WE = W12 + KF * D
NS = 40
SCALE = float(HD) ** -0.5


CONSTS = [("ident", P), ("cos", HD), ("sin", HD), ("iota", P), ("tri", P), ("ones", P), ("mask", P),
          ("thr", 15), ("tok", 32), ("spare", 1)]


def wait_prev(eng, sem, n):
    if isinstance(n, int) and n <= 0:
        return
    eng.wait_ge(sem, n)


def decoder(nc, x, ctxT, w_qkv, w_proj, wkv_wu, wgT, w_moe, consts, x3_dram, out):
    B = x.shape[0] // P
    with ExitStack() as ctx:
        def sb(name, shape, dt=F32):
            return ctx.enter_context(nc.sbuf_tensor(name, shape, dt))

        def ps(name, shape):
            return ctx.enter_context(nc.psum_tensor(name, shape, F32))

        def sem(name):
            return ctx.enter_context(nc.semaphore(name))

        t0 = ps("t0", [P, D])
        vp = ps("vp", [P, D])
        qk_ps = ps("qk_ps", [P, 2, D])
        tp = ps("tp", [P, 2, D])
        so = ps("so", [P, 2, D])

        xres = sb("xres", [P, B, D])
        wbig = sb("wbig", [P, 4 * WE], F32R)
        q3 = KD * 3 * D
        wqkv_hi = wbig[:, 0:q3].rearrange("p (k n) -> p k n", k=KD)
        wqkv_lo = wbig[:, q3:2 * q3].rearrange("p (k n) -> p k n", k=KD)
        wproj_hi = wbig[:, 2 * q3:2 * q3 + KD * D].rearrange("p (k n) -> p k n", k=KD)
        wproj_lo = wbig[:, 2 * q3 + KD * D:2 * q3 + 2 * KD * D].rearrange("p (k n) -> p k n", k=KD)
        wexp = wbig[:].rearrange("p (b s n) -> p b s n", b=2, s=2)
        wraw = sb("wraw", [P, WE])
        cst = sb("cst", [P, consts.shape[1]])
        rot = wraw[:, 0:2 * D].rearrange("p (w n) -> p w n", w=2)
        at = {}
        off = 0
        for name, width in CONSTS:
            at[name] = cst[:, off:off + width]
            off += width
        idm = at["ident"]
        cos_sb, sin_sb = at["cos"], at["sin"]
        wg_sb = sb("wg_sb", [P, KD, E])
        sc_all = sb("sc_all", [P, B, E])
        ids_sb = sb("ids_sb", [P, NS], U32)
        w_sb = sb("w_sb", [P, NS])
        tab = sb("tab", [P, 4, NS], I32)
        nslot = sb("nslot", [P, 1], I32)
        idg = sb("idg", [P, 1], U32)
        ids_out = sb("ids_out", [P, 1], U32)
        holdp = sb("holdp", [P, 3])
        wu_in = sb("wu_in", [P, 2, KD])
        mv1 = sb("mv1", [P, B, 2])
        bst = sb("bst", [P, B, 6])
        ln1 = sb("ln1", [P, B])
        rstd1 = sb("rstd1", [P, B])
        xn = sb("xn", [P, D])
        xnT_hi = sb("xnT_hi", [P, KD, P], F32R)
        xnT_lo = sb("xnT_lo", [P, KD, P], F32R)
        qk = sb("qk", [P, 2, D])
        vext = sb("vext", [P, H, HD + 1])
        qT = sb("qT", [P, KD, P])
        kblk = sb("kblk", [P, KD, HB, P])
        mx = sb("mx", [P, H])
        nb = sb("nb", [P, H])
        rinv = sb("rinv", [P, H])
        o_sb = sb("o_sb", [P, D])
        oT_hi = sb("oT_hi", [P, KD, P], F32R)
        oT_lo = sb("oT_lo", [P, KD, P], F32R)
        mv2 = sb("mv2", [P, 2])
        bst2 = sb("bst2", [P, 6])
        rstd2 = sb("rstd2", [P, 2])
        kn = sb("kn", [P, D])
        kT = sb("kT", [P, D])
        vT = sb("vT", [P, D])
        wtab = sb("wtab", [P, 2, KD, P])
        omax = sb("omax", [P, 1 + D])
        kk = sb("kk", [P, 2, D])
        pq = sb("pq", [P, 2, 1 + D])
        yT = sb("yT", [P, D])
        mv3 = sb("mv3", [P, 2])
        bst3 = sb("bst3", [P, 6])
        rstd3 = sb("rstd3", [P, 2])
        eps_c = sb("eps_c", [P, 1])
        hold = sb("hold", [P, 1])
        x3n = sb("x3n", [P, D])
        scratch = sb("scratch", [P, 4 * 2048])
        wqkv_raw = scratch[:, 0:KD * 3 * D].rearrange("p (k n) -> p k n", k=KD)
        wproj_raw = scratch[:, KD * 3 * D:].rearrange("p (k n) -> p k n", k=KD)
        prob = scratch[:, 0:2048].rearrange("p (h n) -> p h n", h=H)
        probT = scratch[:, 2048:4096].rearrange("p (h n) -> p h n", h=H)
        relu = scratch[:, 4096:6144].rearrange("p (s n) -> p s n", s=4)
        ez = scratch[:, 6144:8192].rearrange("p (s n) -> p s n", s=4)
        apq = relu[:, 0:2]
        x3T = relu[:, 2]
        hsb = qT[:].rearrange("p k n -> p (k n)")[:, 0:KF * P]
        gsb = kT[:, 0:FH]
        ea = kk

        names = """const_in w_tab_in wg_in stats1 mean1 lnv1 rstd1_ok xn_ok xnT_ps xhi xlo q_ps k_ps v_ps
        rope_a rope_b rope_c qk_ok ropeq_read ropek_read v_ok qT_ps kT_ps qT_ok kb_ok zero_ok s_ps
        mx_ok nb_ok exp_ok pt_ps pt_ok pv_ps rinv_ok o_ok oT_ps ohi olo proj_ps x1_ok st2 mv2_ok
        ln2 rs2 kn_ok knT_ps kT_ok vT_in ev_ok tab_ok om_ok kk_ok dm_ok rl_ok ee_ok p_ok q_ok ap_ok
        nd_ok lnd rd_ok y_ok yT_ps x2_ok st3 mv3_ok ln3 rs3 x3_ok x3_out ones_ok wsplit_act wsplit_dve
        out_done wraw_in wlo_ok whi_ok x2_out spare_out x3T_ps x3T_ok sc_ps sc_ok top_ok oh_ok
        ds_ok e12_ok rk_ps sl_ok sel_ok inv_ps tab_set step m_idg m_xg m_xT m_xhi m_xlo m_gu m_silu m_h m_hT
        m_hhi m_hlo m_y m_yok m_sc held held_x held_y""".split()
        s = {n: sem(n) for n in names}
        x_in = [sem(f"x_in{g}") for g in range(4)]
        wq_in = [sem(f"wq_in{k}") for k in range(KD)]
        wp_in = sem("wp_in")

        groups = [(0, 1), (1, 4), (4, 10), (10, B)]
        block = ctx.enter_context(nc.Block())

        def schedule(eng, body):
            for i in range(5):
                body(i, True, i >= 1, i >= 2, i >= 3, i >= 4)
            with eng.Fori(5, B) as i:
                body(i, True, True, True, True, True)
            for i in range(B, B + 4):
                body(i, False, i < B + 1, i < B + 2, i < B + 3, True)

        def slots(eng, body):
            n = eng.value_load(nslot[0:1, 0:1], min_val=E - 3, max_val=NS - 4) + 3
            for k in range(3):
                body(k, True, k >= 1, k >= 2)
            with eng.Fori(3, n) as k:
                body(k, True, True, True)
            body(n, False, True, True)
            body(n + 1, False, False, True)

        def split_next(eng, k, rest):
            starts = eng.value_load(tab[0:1, 2, bass.ds(k - 2, 1)], min_val=0, max_val=1)
            other = eng.value_load(tab[0:1, 3, bass.ds(k - 2, 1)], min_val=0, max_val=1)
            nxt = eng.value_load(tab[0:1, 1, bass.ds(k - 2, 1)], min_val=1, max_val=E)
            with eng.If(starts == 1):
                wait_prev(eng, s["m_y"], k - 2)
                hi = wexp[:, bass.ds(other, 1), 0, :].rearrange("p o n -> p (o n)")
                lo = wexp[:, bass.ds(other, 1), 1, :].rearrange("p o n -> p (o n)")
                if rest:
                    eng.wait_ge(s["whi_ok"], nxt + 1)
                    nc.vector.tensor_tensor(lo, wraw[:], hi.bitcast(F32), ALU.subtract).then_inc(s["wlo_ok"], 1)
                else:
                    eng.wait_ge(s["wraw_in"], 16 * (nxt + 1))
                    nc.scalar.activation(hi, wraw[:], ACT.Copy).then_inc(s["whi_ok"], 1)

        sel_p = wexp[:, 1].rearrange("p s n -> p (s n)")[:, 0:2 * B * P].rearrange("p (a n) -> p a n", n=P)
        sel_v = wexp[:, 1].rearrange("p s n -> p (s n)")[:, 2 * B * P:2 * B * (P + 3 * NS)].rearrange(
            "p (a v n) -> p a v n", v=3, n=NS)
        pos = [0]

        def tmp(*shape):
            n = 1
            for d in shape:
                n *= d
            a = scratch[:, pos[0]:pos[0] + n]
            pos[0] += n
            if len(shape) == 1:
                return a
            names = "abcd"[:len(shape)]
            return a.rearrange(f"p ({' '.join(names)}) -> p {' '.join(names)}", **dict(zip(names, shape)))

        top8, idx8 = tmp(B, 8), tmp(B, 8).bitcast(U32)
        ds12, e12 = tmp(B), tmp(B)
        idxf, oh = tmp(2, B), tmp(2, B, E)
        picked3 = tmp(B, E)
        picked = picked3.rearrange("p b e -> p (b e)")
        vals = tmp(2 * B, 3)

        @block.gpsimd
        def _(pool):
            pool.wait_ge(s["x3_out"], 16 * B)
            pool.wait_ge(s["x2_out"], 16 * B)
            pool.wait_ge(s["spare_out"], 32)
            pool.wait_ge(s["tab_set"], 1)
            nc.gpsimd.memset(holdp[:], 0.0).then_inc(s["held"], 1)
            pool.wait_ge(s["held"], 1)

            def gather():
                nc.gpsimd.indirect_dma_start(xn[:], None, x3_dram, bass.IndirectOffsetOnAxis(ap=idg[:], axis=0)).then_inc(s["m_xg"], 16)

            pool.wait_ge(s["m_idg"], 1)
            gather()

            def carry(c, sem):
                nc.gpsimd.tensor_tensor(holdp[:, c:c + 1], holdp[:, 2:3], holdp[:, 2:3], ALU.add).then_inc(sem, 1)

            def moe(k, X, M1, M2):
                if X:
                    wait_prev(pool, s["held_x"], k)
                    pool.wait_ge(s["m_idg"], k + 2)
                    carry(0, s["held_x"])
                    gather()
                if M2:
                    wait_prev(pool, s["held_y"], k - 2)
                    pool.wait_ge(s["m_yok"], k - 1)
                    carry(1, s["held_y"])
                    nc.gpsimd.indirect_dma_start(out, bass.IndirectOffsetOnAxis(ap=ids_out[:], axis=0), o_sb[:], None,
                                                 compute_op=ALU.add).then_inc(s["m_sc"], 16)
            slots(pool, moe)
            n = pool.value_load(nslot[0:1, 0:1], min_val=E - 3, max_val=NS - 4) + 3
            pool.wait_ge(s["m_sc"], 16 * n)
            pool.wait_ge(s["m_xg"], 16 * (n + 1))

        @block.sync
        def _(sp):
            sp.dma_start(cst[:], consts).then_inc(s["const_in"], 16)
            xv = x.rearrange("(b t) d -> t b d", t=P)
            sp.dma_start(xres[:, 0:1, :], xv[:, 0:1, :]).then_inc(x_in[0], 16)
            for k in range(KD):
                sp.dma_start(wqkv_raw[:, k, :], w_qkv[k * P:(k + 1) * P, :]).then_inc(wq_in[k], 16)
            sp.dma_start(wproj_raw, w_proj.rearrange("(k p) n -> p k n", p=P)).then_inc(wp_in, 16)
            sp.dma_start(wg_sb[:], wgT).then_inc(s["wg_in"], 16)
            sp.dma_start(wu_in[:], wkv_wu).then_inc(s["w_tab_in"], 16)
            for g, (a, b) in enumerate(groups[1:]):
                sp.dma_start(xres[:, a:b, :], xv[:, a:b, :]).then_inc(x_in[g + 1], 16)
            sp.wait_ge(s["zero_ok"], 1)
            sp.dma_start(x3_dram[B * P:B * P + P, :], o_sb[:]).then_inc(s["spare_out"], 16)
            sp.dma_start(out[B * P:B * P + P, :], o_sb[:]).then_inc(s["spare_out"], 16)

            def body(i, A, Bs, U, C, Ds):
                if C:
                    c = i - 3
                    wait_prev(sp, s["ev_ok"], c)
                    sp.dma_start(vT[:].rearrange("p (k t) -> p k t", k=KD), ctxT[bass.ds(c, 1)].rearrange("o p k t -> p (o k) t")).then_inc(s["vT_in"], 16)
                if Ds:
                    e = i - 4
                    sp.wait_ge(s["x2_ok"], e + 1)
                    sp.dma_start(out[bass.ds(e * P, P), :], xres[:, bass.ds(e, 1), :].rearrange("p o n -> p (o n)")).then_inc(s["x2_out"], 16)
                    sp.wait_ge(s["x3_ok"], e + 1)
                    sp.dma_start(x3_dram[bass.ds(e * P, P), :], x3n[:]).then_inc(s["x3_out"], 16)
            schedule(sp, body)
            sp.wait_ge(s["qk_ok"], 2 * B)
            for e in range(E):
                wait_prev(sp, s["wlo_ok"], e)
                sp.dma_start(wraw[:], w_moe[e]).then_inc(s["wraw_in"], 16)
            sp.wait_ge(s["x2_out"], 16 * B)
            sp.wait_ge(s["x3_out"], 16 * B)

        @block.tensor
        def _(pe):
            def three(dst, k, hi, lo, w_hi, w_lo, first, last):
                pe.matmul(dst, hi[:, k, :], w_hi, start=first, stop=False)
                pe.matmul(dst, hi[:, k, :], w_lo, start=False, stop=False)
                return pe.matmul(dst, lo[:, k, :], w_hi, start=False, stop=last)

            def turn(dst, src):
                for k in range(KD):
                    mm = pe.transpose(dst[:, k * P:(k + 1) * P], src[:, k * P:(k + 1) * P], idm)
                return mm

            def project(dst, hi, lo, w_hi, w_lo, a):
                for k in range(KD):
                    mm = three(dst, k, hi, lo, w_hi[:, k, a:a + D], w_lo[:, k, a:a + D], k == 0, k == KD - 1)
                return mm

            pe.wait_ge(s["const_in"], 16)

            def body(i, A, Bs, U, C, Ds):
                t, u, c, e = i - 1, i - 2, i - 3, i - 4

                def score(j):
                    pe.matmul(so[:, j % 2, :], qT[:, j, :], kblk[:, j].rearrange("p r n -> p (r n)"),
                              start=True, stop=True).then_inc(s["s_ps"], 1)

                def turn_prob(j):
                    pe.wait_ge(s["exp_ok"], 4 * t + j + 1)
                    for r in range(HB):
                        mm = pe.transpose(tp[:, j % 2, r * P:(r + 1) * P], prob[:, HB * j + r, :], idm)
                    mm.then_inc(s["pt_ps"], 1)

                def pv(j):
                    for r in range(HB):
                        h = HB * j + r
                        a = (h % 8) * (HD + 1)
                        mm = pe.matmul(so[:, h // 8, a:a + HD + 1], probT[:, h, :], vext[:, h, :], start=True, stop=True)
                    mm.then_inc(s["pv_ps"], 1)

                if Bs:
                    pe.wait_ge(s["qk_ok"], 2 * t + 2)
                    wait_prev(pe, s["pt_ok"], 4 * t)
                    turn(tp[:, 0, :], qk[:, 0, :]).then_inc(s["qT_ps"], 1)
                    turn(tp[:, 1, :], qk[:, 1, :]).then_inc(s["kT_ps"], 1)
                if Ds:
                    pe.wait_ge(s["y_ok"], e + 1)
                    if isinstance(i, int) and i == 4:
                        pe.wait_ge(s["kT_ok"], 1)
                    else:
                        pe.wait_ge(s["sc_ok"], e)
                    turn(t0[:], yT).then_inc(s["yT_ps"], 1)
                if Bs:
                    if isinstance(i, int) and i <= 2:
                        wait_prev(pe, s["v_ok"], t)
                    else:
                        pe.wait_ge(s["x1_ok"], i - 2)
                    project(vp[:], xnT_hi, xnT_lo, wqkv_hi, wqkv_lo, 2 * D).then_inc(s["v_ps"], 1)
                if A:
                    pe.wait_ge(s["xn_ok"], i + 1)
                    if Ds:
                        pe.wait_ge(s["x2_ok"], e + 1)
                    else:
                        wait_prev(pe, s["xlo"], i)
                    turn(t0[:], xn).then_inc(s["xnT_ps"], 1)
                if Bs:
                    pe.wait_ge(s["qT_ok"], t + 1)
                    pe.wait_ge(s["kb_ok"], 4 * t + 4)
                    wait_prev(pe, s["o_ok"], 2 * t)
                    score(0)
                    score(1)
                if U:
                    pe.wait_ge(s["o_ok"], 2 * u + 2)
                    if Bs:
                        pe.wait_ge(s["v_ok"], t + 1)
                    else:
                        pe.wait_ge(s["x1_ok"], u)
                    turn(vp[:], o_sb).then_inc(s["oT_ps"], 1)
                if A:
                    if isinstance(i, int) and i == 0:
                        pe.wait_ge(s["wsplit_dve"], KD)
                        pe.wait_ge(s["wsplit_act"], KD)
                    pe.wait_ge(s["xhi"], i + 1)
                    pe.wait_ge(s["xlo"], i + 1)
                    wait_prev(pe, s["ropeq_read"], 2 * i)
                    project(qk_ps[:, 0, :], xnT_hi, xnT_lo, wqkv_hi, wqkv_lo, 0).then_inc(s["q_ps"], 1)
                if Bs:
                    pe.wait_ge(s["exp_ok"], 4 * t + 1)
                    score(2)
                    turn_prob(0)
                    pe.wait_ge(s["exp_ok"], 4 * t + 2)
                    score(3)
                    turn_prob(1)
                if U:
                    if isinstance(i, int) and i == 2:
                        pe.wait_ge(s["wsplit_dve"], KD + 1)
                        pe.wait_ge(s["wsplit_act"], KD + 1)
                    pe.wait_ge(s["ohi"], u + 1)
                    pe.wait_ge(s["olo"], u + 1)
                    project(vp[:], oT_hi, oT_lo, wproj_hi, wproj_lo, 0).then_inc(s["proj_ps"], 1)
                if C:
                    pe.wait_ge(s["kn_ok"], c + 1)
                    if A:
                        pe.wait_ge(s["xlo"], i + 1)
                    else:
                        pe.wait_ge(s["x2_ok"], e + 1)
                    turn(t0[:], kn).then_inc(s["knT_ps"], 1)
                if Bs:
                    pe.wait_ge(s["pt_ok"], 4 * t + 1)
                    turn_prob(2)
                    pe.wait_ge(s["pt_ok"], 4 * t + 2)
                    turn_prob(3)
                if A:
                    wait_prev(pe, s["ropek_read"], 2 * i)
                    project(qk_ps[:, 1, :], xnT_hi, xnT_lo, wqkv_hi, wqkv_lo, D).then_inc(s["k_ps"], 1)
                if Ds:
                    pe.wait_ge(s["x3_ok"], e + 1)
                    if C:
                        pe.wait_ge(s["kT_ok"], c + 1)
                    turn(t0[:], x3n).then_inc(s["x3T_ps"], 1)
                if Bs:
                    for j in range(KD):
                        pe.wait_ge(s["pt_ok"], 4 * t + j + 1)
                        pv(j)
                if Ds:
                    if isinstance(i, int) and i == 4:
                        pe.wait_ge(s["wg_in"], 16)
                    pe.wait_ge(s["x3T_ok"], e + 1)
                    for k in range(KD):
                        mm = pe.matmul(t0[:, 0:E], x3T[:, k * P:(k + 1) * P], wg_sb[:, k, :], start=k == 0, stop=k == KD - 1)
                    mm.then_inc(s["sc_ps"], 1)
            schedule(pe, body)

            pe.wait_ge(s["oh_ok"], 3)
            pe.matmul(t0[:, 0:P], at["tri"], picked, start=True, stop=True)
            pe.matmul(t0[:, P:2 * P], at["ones"], picked, start=True, stop=True).then_inc(s["rk_ps"], 1)
            pe.wait_ge(s["sel_ok"], 2)
            for a in range(2 * B):
                mm = pe.matmul(vp[:, 0:3 * NS], sel_p[:, a, :], sel_v[:, a].rearrange("p v n -> p (v n)"),
                               start=a == 0, stop=a == 2 * B - 1)
            mm.then_inc(s["inv_ps"], 1)

            pe.wait_ge(s["tab_set"], 1)

            def moe(k, X, M1, M2):
                if M1:
                    par1 = pe.value_load(tab[0:1, 0, bass.ds(k - 1, 1)], min_val=0, max_val=1)
                    need = pe.value_load(tab[0:1, 1, bass.ds(k - 1, 1)], min_val=1, max_val=E)
                if M2:
                    par2 = pe.value_load(tab[0:1, 0, bass.ds(k - 2, 1)], min_val=0, max_val=1)
                    pe.wait_ge(s["m_h"], k - 1)
                    wait_prev(pe, s["m_hlo"], k - 2)
                    for f in range(KF):
                        n = min(P, FH - f * P)
                        mm = pe.transpose(vp[0:n, f * P:(f + 1) * P], hsb[:, f * P:f * P + n], idm)
                    mm.then_inc(s["m_hT"], 1)
                if X:
                    pe.wait_ge(s["m_xg"], 16 * (k + 1))
                    wait_prev(pe, s["m_xlo"], k)
                    turn(t0[:], xn).then_inc(s["m_xT"], 1)
                if M1:
                    pe.wait_ge(s["wlo_ok"], need)
                    pe.wait_ge(s["m_xlo"], k)
                    wait_prev(pe, s["m_h"], k - 1)
                    for g in range(2):
                        for f in range(KD):
                            a = f * 2 * FH + g * FH
                            w_hi = wexp[:, bass.ds(par1, 1), 0, a:a + FH].rearrange("p o n -> p (o n)")
                            w_lo = wexp[:, bass.ds(par1, 1), 1, a:a + FH].rearrange("p o n -> p (o n)")
                            mm = three(qk_ps[:, g, 0:FH], f, xnT_hi, xnT_lo, w_hi, w_lo, f == 0, f == KD - 1)
                    mm.then_inc(s["m_gu"], 1)
                if M2:
                    pe.wait_ge(s["m_hlo"], k - 1)
                    wait_prev(pe, s["m_yok"], k - 2)
                    for f in range(KF):
                        n = min(P, FH - f * P)
                        a = W12 + f * D
                        w_hi = wexp[0:n, bass.ds(par2, 1), 0, a:a + D].rearrange("p o n -> p (o n)")
                        w_lo = wexp[0:n, bass.ds(par2, 1), 1, a:a + D].rearrange("p o n -> p (o n)")
                        mm = three(tp[:, 0, :], f, oT_hi[0:n], oT_lo[0:n], w_hi, w_lo, f == 0, f == KF - 1)
                    mm.then_inc(s["m_y"], 1)
            slots(pe, moe)

        @block.scalar
        def _(act):
            nc.scalar.preload_act_table_set("natural_log_exp_and_others")
            for k in range(KD):
                act.wait_ge(wq_in[k], 16)
                nc.scalar.activation(wqkv_hi[:, k, :], wqkv_raw[:, k, :], ACT.Copy).then_inc(s["wsplit_act"], 1)
            act.wait_ge(wp_in, 16)
            nc.scalar.activation(wproj_hi, wproj_raw, ACT.Copy).then_inc(s["wsplit_act"], 1)
            for g, (a, b) in enumerate(groups):
                act.wait_ge(s["mean1"], b)
                nc.scalar.activation(ln1[:, a:b], mv1[:, a:b, 1], ACT.Ln, bias=eps_c[:, 0:1]).then_inc(s["lnv1"], 1)
                act.wait_ge(s["lnv1"], g + 1)
                nc.scalar.activation(rstd1[:, a:b], ln1[:, a:b], ACT.Exp, scale=-0.5).then_inc(s["rstd1_ok"], 1)

            def body(i, A, Bs, U, C, Ds):
                t, u, c, e = i - 1, i - 2, i - 3, i - 4

                def exps(j):
                    act.wait_ge(s["nb_ok"], 4 * t + j + 1)
                    wait_prev(act, s["pt_ps"], 4 * t + j - 3 if not isinstance(t, int) or t > 0 else 0)
                    for r in range(HB):
                        h = HB * j + r
                        a = nc.scalar.activation(prob[:, h, :], so[:, j % 2, r * P:(r + 1) * P], ACT.Exp,
                                                 bias=nb[:, h:h + 1], scale=SCALE)
                    a.then_inc(s["exp_ok"], 1)

                def take_prob(j):
                    act.wait_ge(s["pt_ps"], 4 * t + j + 1)
                    wait_prev(act, s["pv_ps"], 4 * t if not isinstance(t, int) or t > 0 else 0)
                    nc.scalar.activation(probT[:, HB * j:HB * j + HB, :].rearrange("p h n -> p (h n)"),
                                         tp[:, j % 2, :], ACT.Copy).then_inc(s["pt_ok"], 1)

                if Bs:
                    act.wait_ge(s["kT_ps"], t + 1)
                    if isinstance(i, int) and i == 1:
                        act.wait_ge(s["zero_ok"], 1)
                    for r in range(HB):
                        nc.scalar.activation(kblk[HD * r:HD * r + HD, :, r, :],
                                             tp[HD * r:HD * r + HD, 1, :].rearrange("p (k n) -> p k n", k=KD),
                                             ACT.Copy).then_inc(s["kb_ok"], 1)
                    act.wait_ge(s["v_ps"], t + 1)
                    wait_prev(act, s["pv_ps"], 4 * t)
                    nc.scalar.activation(vext[:, :, 0:HD], vp[:].rearrange("p (h d) -> p h d", h=H),
                                         ACT.Copy).then_inc(s["v_ok"], 1)
                if A:
                    act.wait_ge(s["xnT_ps"], i + 1)
                    wait_prev(act, s["v_ps"], i)
                    nc.scalar.activation(xnT_hi[:].rearrange("p k n -> p (k n)"), t0[:], ACT.Copy).then_inc(s["xhi"], 1)
                if Ds:
                    act.wait_ge(s["mv3_ok"], e + 1)
                    nc.scalar.activation(rstd3[:, 0:1], mv3[:, 1:2], ACT.Ln, bias=eps_c[:, 0:1]).then_inc(s["ln3"], 1)
                    act.wait_ge(s["ln3"], e + 1)
                    nc.scalar.activation(rstd3[:, 1:2], rstd3[:, 0:1], ACT.Exp, scale=-0.5).then_inc(s["rs3"], 1)
                if Bs:
                    exps(0)
                    exps(1)
                if U:
                    act.wait_ge(s["oT_ps"], u + 1)
                    wait_prev(act, s["proj_ps"], u)
                    nc.scalar.activation(oT_hi[:].rearrange("p k n -> p (k n)"), vp[:], ACT.Copy).then_inc(s["ohi"], 1)
                if Bs:
                    take_prob(0)
                    take_prob(1)
                    exps(2)
                if C:
                    act.wait_ge(s["knT_ps"], c + 1)
                    wait_prev(act, s["kk_ok"], c)
                    nc.scalar.activation(kT[:], t0[:], ACT.Copy).then_inc(s["kT_ok"], 1)
                if Bs:
                    exps(3)
                    take_prob(2)
                if U:
                    act.wait_ge(s["mv2_ok"], u + 1)
                    nc.scalar.activation(rstd2[:, 0:1], mv2[:, 1:2], ACT.Ln, bias=eps_c[:, 0:1]).then_inc(s["ln2"], 1)
                    act.wait_ge(s["ln2"], u + 1)
                    nc.scalar.activation(rstd2[:, 1:2], rstd2[:, 0:1], ACT.Exp, scale=-0.5).then_inc(s["rs2"], 1)
                if Bs:
                    take_prob(3)
                if C:
                    act.wait_ge(s["dm_ok"], c + 1)
                    wait_prev(act, s["sc_ps"], c - 1)
                    nc.scalar.activation(relu[:, 0:2, :], kk[:], ACT.Relu, scale=-1.0).then_inc(s["rl_ok"], 1)
                    nc.scalar.activation(relu[:, 2:4, :], kk[:], ACT.Relu).then_inc(s["rl_ok"], 1)
                    act.wait_ge(s["rl_ok"], 2 * c + 2)
                    wait_prev(act, s["nd_ok"], c)
                    nc.scalar.activation(ea[:], relu[:, 0:2, :], ACT.Exp, scale=-1.0).then_inc(s["ee_ok"], 1)
                    nc.scalar.activation(ez[:].rearrange("p (a b) n -> p a b n", b=2)[:, :, 1, :], relu[:, 2:4, :],
                                         ACT.Exp, scale=-1.0).then_inc(s["ee_ok"], 1)
                if Ds:
                    act.wait_ge(s["x3T_ps"], e + 1)
                    wait_prev(act, s["sc_ps"], e)
                    if C:
                        act.wait_ge(s["ee_ok"], 2 * c + 2)
                    nc.scalar.activation(x3T, t0[:], ACT.Copy).then_inc(s["x3T_ok"], 1)
                if C:
                    act.wait_ge(s["nd_ok"], c + 1)
                    nc.scalar.activation(kk[:, 0, :], apq[:, 1, :], ACT.Ln).then_inc(s["lnd"], 1)
                    act.wait_ge(s["lnd"], c + 1)
                    nc.scalar.activation(kk[:, 1, :], kk[:, 0, :], ACT.Exp, scale=-1.0).then_inc(s["rd_ok"], 1)
            schedule(act, body)

            act.wait_ge(s["ds_ok"], 1)
            nc.scalar.activation(e12, ds12, ACT.Exp).then_inc(s["e12_ok"], 1)
            act.wait_ge(s["wraw_in"], 16)
            nc.scalar.activation(wexp[:, 0, 0, :], wraw[:], ACT.Copy).then_inc(s["whi_ok"], 1)
            act.wait_ge(s["tab_set"], 1)

            def moe(k, X, M1, M2):
                if M2:
                    split_next(act, k, False)
                    act.wait_ge(s["m_hT"], k - 1)
                    wait_prev(act, s["m_y"], k - 2)
                    nc.scalar.activation(oT_hi[:, 0:KF, :].rearrange("p k n -> p (k n)"), vp[:, 0:KF * P],
                                         ACT.Copy).then_inc(s["m_hhi"], 1)
                if M1:
                    act.wait_ge(s["m_gu"], k)
                    wait_prev(act, s["m_h"], k - 1)
                    nc.scalar.activation(gsb, qk_ps[:, 0, 0:FH], ACT.Silu).then_inc(s["m_silu"], 1)
                if X:
                    act.wait_ge(s["m_xT"], k + 1)
                    wait_prev(act, s["m_gu"], k)
                    nc.scalar.activation(xnT_hi[:].rearrange("p k n -> p (k n)"), t0[:], ACT.Copy).then_inc(s["m_xhi"], 1)
            slots(act, moe)

        @block.vector
        def _(dve):
            v = nc.vector
            v.memset(eps_c[:], EPS)
            for tile in (kblk, omax, pq, o_sb):
                v.memset(tile[:], 0.0)
            v.memset(vext[:, :, HD:HD + 1], 1.0).then_inc(s["zero_ok"], 1)
            dve.wait_ge(s["zero_ok"], 1)
            for g, (lo, hi) in enumerate(groups):
                dve.wait_ge(x_in[g], 16)
                for b in range(lo, hi):
                    v.bn_stats(bst[:, b, :], xres[:, b, :]).then_inc(s["stats1"], 1)
                    dve.wait_ge(s["stats1"], b + 1)
                    v.bn_aggr(mv1[:, b, :], bst[:, b, :]).then_inc(s["mean1"], 1)
                if g == 0:
                    for k in range(KD):
                        dve.wait_ge(s["wsplit_act"], k + 1)
                        v.tensor_tensor(wqkv_lo[:, k, :], wqkv_raw[:, k, :], wqkv_hi[:, k, :].bitcast(F32),
                                        ALU.subtract).then_inc(s["wsplit_dve"], 1)
                    dve.wait_ge(s["wsplit_act"], KD + 1)
                    v.tensor_tensor(wproj_lo, wproj_raw, wproj_hi.bitcast(F32),
                                    ALU.subtract).then_inc(s["wsplit_dve"], 1)
            dve.wait_ge(s["w_tab_in"], 16)
            v.tensor_copy(wtab[:, 0], wu_in[:, 0, :].rearrange("p (k o) -> p k o", o=1).broadcast_to([P, KD, P])).then_inc(s["tab_ok"], 1)
            v.tensor_scalar(wtab[:, 1], wu_in[:, 1, :].rearrange("p (k o) -> p k o", o=1).broadcast_to([P, KD, P]),
                            -1.0, None, ALU.mult).then_inc(s["tab_ok"], 1)
            dve.wait_ge(s["tab_ok"], 2)
            v.memset(wtab[:, :, :, 0:1], NEG).then_inc(s["tab_ok"], 1)
            dve.wait_ge(s["tab_ok"], 3)
            dve.wait_ge(s["const_in"], 16)

            def normalise(dst, src, mean, rstd):
                return v.tensor_scalar(dst, src, mean, rstd, ALU.subtract, ALU.mult)

            def body(i, A, Bs, U, C, Ds):
                t, u, c, e = i - 1, i - 2, i - 3, i - 4

                def maxes(j):
                    dve.wait_ge(s["s_ps"], 4 * t + j + 1)
                    v.tensor_reduce(mx[:, HB * j:HB * j + HB], so[:, j % 2, :].rearrange("p (r n) -> p r n", r=HB),
                                    AX_X, ALU.max).then_inc(s["mx_ok"], 1)
                    dve.wait_ge(s["mx_ok"], 4 * t + j + 1)
                    v.tensor_scalar(nb[:, HB * j:HB * j + HB], mx[:, HB * j:HB * j + HB], -SCALE, None,
                                    ALU.mult).then_inc(s["nb_ok"], 1)

                def rope(w, ready, read):
                    dve.wait_ge(s[ready], i + 1)
                    src = qk_ps[:, w, :].rearrange("p (h d) -> p h d", h=H)
                    cosb = cos_sb.rearrange("p (o d) -> p o d", o=1).broadcast_to([P, H, HD])
                    v.tensor_tensor(rot[:, w, :].rearrange("p (h d) -> p h d", h=H), src, cosb,
                                    ALU.mult).then_inc(s["rope_a"], 1)
                    s4 = qk_ps[:, w, :].rearrange("p (h d two) -> p h d two", h=H, two=2)
                    d4 = qk[:, w, :].rearrange("p (h d two) -> p h d two", h=H, two=2)
                    for a in range(2):
                        sn = sin_sb.rearrange("p (o d two) -> p o d two", o=1, two=2)[:, :, :, a].broadcast_to([P, H, HD // 2])
                        v.tensor_tensor(d4[:, :, :, a], s4[:, :, :, 1 - a], sn, ALU.mult).then_inc(s[read], 1)
                    dve.wait_ge(s["rope_a"], 2 * i + w + 1)
                    dve.wait_ge(s[read], 2 * i + 2)
                    v.tensor_tensor(qk[:, w, :], qk[:, w, :], rot[:, w, :], ALU.add).then_inc(s["qk_ok"], 1)

                if Ds:
                    dve.wait_ge(s["rd_ok"], e + 1)
                    wait_prev(dve, s["yT_ps"], e)
                    v.tensor_tensor(yT[:], apq[:, 0, :], kk[:, 1, :], ALU.mult).then_inc(s["y_ok"], 1)
                if A:
                    if isinstance(i, int):
                        dve.wait_ge(s["rstd1_ok"], sum(i >= a for a, b in groups))
                    elif A:
                        dve.wait_ge(s["rstd1_ok"], len(groups))
                    wait_prev(dve, s["xnT_ps"], i)
                    normalise(xn[:], xres[:, bass.ds(i, 1), :].rearrange("p o n -> p (o n)"), mv1[:, bass.ds(i, 1), 0], rstd1[:, bass.ds(i, 1)]).then_inc(s["xn_ok"], 1)
                if Bs:
                    dve.wait_ge(s["qT_ps"], t + 1)
                    v.tensor_copy(qT[:].rearrange("p k n -> p (k n)"), tp[:, 0, :]).then_inc(s["qT_ok"], 1)
                if Ds:
                    xr = xres[:, bass.ds(e, 1), :].rearrange("p o n -> p (o n)")
                    dve.wait_ge(s["yT_ps"], e + 1)
                    v.tensor_tensor(xr, xr, t0[:], ALU.add).then_inc(s["x2_ok"], 1)
                    dve.wait_ge(s["x2_ok"], e + 1)
                    v.memset(hold[:], 0.0)
                    v.bn_stats(bst3[:], xr).then_inc(s["st3"], 1)
                    dve.wait_ge(s["st3"], e + 1)
                    v.memset(hold[:], 0.0)
                    v.bn_aggr(mv3[:], bst3[:]).then_inc(s["mv3_ok"], 1)
                if A:
                    dve.wait_ge(s["xhi"], i + 1)
                    v.tensor_tensor(xnT_lo[:].rearrange("p k n -> p (k n)"), t0[:],
                                    xnT_hi[:].rearrange("p k n -> p (k n)").bitcast(F32), ALU.subtract).then_inc(s["xlo"], 1)
                if Bs:
                    maxes(0)
                    maxes(1)
                if Ds:
                    dve.wait_ge(s["rs3"], e + 1)
                    wait_prev(dve, s["x3_out"], 16 * e)
                    normalise(x3n[:], xr, mv3[:, 0:1], rstd3[:, 1:2]).then_inc(s["x3_ok"], 1)
                if U:
                    dve.wait_ge(s["ohi"], u + 1)
                    v.tensor_tensor(oT_lo[:].rearrange("p k n -> p (k n)"), vp[:],
                                    oT_hi[:].rearrange("p k n -> p (k n)").bitcast(F32), ALU.subtract).then_inc(s["olo"], 1)
                if A:
                    rope(0, "q_ps", "ropeq_read")
                if Bs:
                    maxes(2)
                    maxes(3)
                if U:
                    xu = xres[:, bass.ds(u, 1), :].rearrange("p o n -> p (o n)")
                    dve.wait_ge(s["proj_ps"], u + 1)
                    v.tensor_tensor(xu, xu, vp[:], ALU.add).then_inc(s["x1_ok"], 1)
                    dve.wait_ge(s["x1_ok"], u + 1)
                    v.memset(hold[:], 0.0)
                    v.bn_stats(bst2[:], xu).then_inc(s["st2"], 1)
                    dve.wait_ge(s["st2"], u + 1)
                    v.memset(hold[:], 0.0)
                    v.bn_aggr(mv2[:], bst2[:]).then_inc(s["mv2_ok"], 1)
                if C:
                    dve.wait_ge(s["kT_ok"], c + 1)
                    v.tensor_tensor_scan(omax[:, 1:], wtab[:, 0].rearrange("p k n -> p (k n)"), kT[:], 0.0, ALU.add, ALU.max).then_inc(s["om_ok"], 1)
                    v.tensor_tensor(kk[:], kT[:].rearrange("p (o n) -> p o n", o=1).broadcast_to([P, 2, D]),
                                    wtab[:].rearrange("p a k n -> p a (k n)"), ALU.subtract).then_inc(s["kk_ok"], 1)
                    dve.wait_ge(s["om_ok"], c + 1)
                    dve.wait_ge(s["kk_ok"], c + 1)
                    v.tensor_tensor(kk[:], omax[:, 0:D].rearrange("p (o n) -> p o n", o=1).broadcast_to([P, 2, D]),
                                    kk[:], ALU.subtract).then_inc(s["dm_ok"], 1)
                if U:
                    dve.wait_ge(s["rs2"], u + 1)
                    wait_prev(dve, s["knT_ps"], u)
                    normalise(kn[:], xu, mv2[:, 0:1], rstd2[:, 1:2]).then_inc(s["kn_ok"], 1)
                if A:
                    rope(1, "k_ps", "ropek_read")
                if C:
                    ez4 = ez[:].rearrange("p (a b) n -> p a b n", b=2)
                    dve.wait_ge(s["ee_ok"], 2 * c + 2)
                    dve.wait_ge(s["vT_in"], 16 * (c + 1))
                    v.tensor_tensor(ez4[:, :, 0, :], ez4[:, :, 1, :],
                                    vT[:].rearrange("p (o n) -> p o n", o=1).broadcast_to([P, 2, D]), ALU.mult).then_inc(s["ev_ok"], 1)
                    v.tensor_tensor_scan(pq[:, 1, 1:], ea[:, 0, :], ez[:, 1, :], 0.0, ALU.mult, ALU.add).then_inc(s["q_ok"], 1)
                    dve.wait_ge(s["ev_ok"], c + 1)
                    v.tensor_tensor_scan(pq[:, 0, 1:], ea[:, 0, :], ez[:, 0, :], 0.0, ALU.mult, ALU.add).then_inc(s["p_ok"], 1)
                    dve.wait_ge(s["p_ok"], c + 1)
                    dve.wait_ge(s["q_ok"], c + 1)
                    v.tensor_tensor(apq, pq[:, :, 0:D], ea[:, 1, :].rearrange("p (o n) -> p o n", o=1).broadcast_to([P, 2, D]),
                                    ALU.mult).then_inc(s["ap_ok"], 1)
                    dve.wait_ge(s["ap_ok"], c + 1)
                    v.tensor_tensor(apq, apq, ez[:, 2:4, :], ALU.add).then_inc(s["nd_ok"], 1)
                if Bs:
                    for half in range(2):
                        dve.wait_ge(s["pv_ps"], 4 * t + 2 * half + 2)
                        ov = so[:, half, 0:8 * (HD + 1)].rearrange("p (h d) -> p h d", h=8)
                        v.reciprocal(rinv[:, 8 * half:8 * half + 8], ov[:, :, HD]).then_inc(s["rinv_ok"], 1)
                        dve.wait_ge(s["rinv_ok"], 2 * t + half + 1)
                        wait_prev(dve, s["oT_ps"], t)
                        if isinstance(i, int) and i == 1:
                            dve.wait_ge(s["spare_out"], 32)
                        v.tensor_tensor(o_sb[:, half * D // 2:(half + 1) * D // 2].rearrange("p (h d) -> p h d", h=8),
                                        ov[:, :, 0:HD],
                                        rinv[:, 8 * half:8 * half + 8].rearrange("p (h o) -> p h o", o=1).broadcast_to([P, 8, HD]),
                                        ALU.mult).then_inc(s["o_ok"], 1)
                if Ds:
                    dve.wait_ge(s["sc_ps"], e + 1)
                    v.tensor_scalar(sc_all[:, bass.ds(e, 1), :].rearrange("p o n -> p (o n)"), t0[:, 0:E], 0.0, None,
                                    ALU.add).then_inc(s["sc_ok"], 1)
            schedule(dve, body)

            nstep = [0]

            def then(ins):
                nstep[0] += 1
                ins.then_inc(s["step"], 1)
                dve.wait_ge(s["step"], nstep[0])

            dve.wait_ge(s["sc_ok"], B)
            for b in range(B):
                v.max(top8[:, b, :], sc_all[:, b, :]).then_inc(s["top_ok"], 1)
            for b in range(B):
                dve.wait_ge(s["top_ok"], b + 1)
                v.max_index(idx8[:, b, :], top8[:, b, :], sc_all[:, b, :]).then_inc(s["step"], 1)
            nstep[0] += B
            dve.wait_ge(s["top_ok"], B)
            v.tensor_tensor(ds12, top8[:, :, 1], top8[:, :, 0], ALU.subtract).then_inc(s["ds_ok"], 1)
            dve.wait_ge(s["step"], nstep[0])
            then(v.tensor_copy(idxf, idx8[:, :, 0:2].rearrange("p b k -> p k b")))
            expert = at["iota"][:, 0:E].rearrange("p (o e) -> p o e", o=1)
            dve.wait_ge(s["const_in"], 16)
            for a in range(2):
                v.tensor_tensor(oh[:, a], expert.broadcast_to([P, B, E]),
                                idxf[:, a].rearrange("p (b o) -> p b o", o=1).broadcast_to([P, B, E]), ALU.is_equal).then_inc(s["oh_ok"], 1)
            dve.wait_ge(s["oh_ok"], 2)
            v.tensor_tensor(picked3, oh[:, 0], oh[:, 1], ALU.add).then_inc(s["oh_ok"], 1)
            dve.wait_ge(s["e12_ok"], 1)
            den, pk = tmp(B), tmp(2, B)
            then(v.tensor_scalar(den, e12, 1.0, None, ALU.add))
            then(v.reciprocal(pk[:, 0], den))
            then(v.tensor_tensor(pk[:, 1], pk[:, 0], e12, ALU.mult))
            phi = sb("phi", [P, 2 * B], F32R)
            pkf = pk.rearrange("p k b -> p (k b)")
            v.tensor_copy(vals[:, :, 0], at["tok"])
            then(v.tensor_copy(phi[:], pkf))
            v.tensor_copy(vals[:, :, 1], phi[:].bitcast(F32))
            then(v.tensor_tensor(vals[:, :, 2], pkf, phi[:].bitcast(F32), ALU.subtract))
            dve.wait_ge(s["rk_ps"], 1)
            tot, cum, cmp, cnt, last, first = tmp(E, B), tmp(E, B), tmp(E, B - 1), tmp(E), tmp(E), tmp(E)
            then(v.tensor_copy(tot, t0[:, P:2 * P].rearrange("p (b e) -> p e b", e=E)))
            then(v.tensor_tensor_scan(cum.rearrange("p e b -> p (e b)"), at["mask"], tot.rearrange("p e b -> p (e b)"),
                                      0.0, ALU.mult, ALU.add))
            then(v.tensor_tensor(cmp, cum[:, :, B - 1:B].broadcast_to([P, E, B - 1]),
                                 at["thr"].rearrange("p (o n) -> p o n", o=1).broadcast_to([P, E, B - 1]), ALU.is_gt))
            then(v.tensor_reduce(cnt, cmp, AX_X, ALU.add))
            then(v.tensor_scalar(cnt, cnt, 1.0, None, ALU.add))
            then(v.tensor_tensor_scan(last, at["ones"][:, 0:E], cnt, 0.0, ALU.mult, ALU.add))
            then(v.tensor_tensor(first, last, cnt, ALU.subtract))
            then(v.tensor_tensor(cum, cum, tot, ALU.subtract))
            then(v.tensor_scalar(first, first, float(P), None, ALU.mult))
            then(v.tensor_tensor(cum, cum, first.rearrange("p (e o) -> p e o", o=1).broadcast_to([P, E, B]), ALU.add))
            sl, pr, row = tmp(B, E), tmp(2, B * E), tmp(2 * B)
            then(v.tensor_tensor(sl, t0[:, 0:P].rearrange("p (b e) -> p b e", e=E), cum.rearrange("p e b -> p b e"), ALU.add))
            then(v.tensor_tensor(pr, oh.rearrange("p a b e -> p a (b e)"),
                                 sl.rearrange("p b e -> p (b e)").rearrange("p (o n) -> p o n", o=1).broadcast_to([P, 2, B * E]), ALU.mult))
            then(v.tensor_reduce(row, pr.rearrange("p a (b e) -> p (a b) e", e=E), AX_X, ALU.add))
            rowi = tmp(2 * B).bitcast(I32)
            divi, modi = tmp(2 * B).bitcast(I32), tmp(2 * B).bitcast(I32)
            divf, modf = tmp(2 * B), tmp(2 * B)
            then(v.tensor_copy(rowi, row))
            v.tensor_scalar(divi, rowi, 7, None, ALU.logical_shift_right)
            then(v.tensor_scalar(modi, rowi, P - 1, None, ALU.bitwise_and))
            v.tensor_copy(divf, divi)
            then(v.tensor_copy(modf, modi))
            one_s = tmp(2 * B, NS)
            then(v.tensor_tensor(one_s, at["iota"][:, 0:NS].rearrange("p (o n) -> p o n", o=1).broadcast_to([P, 2 * B, NS]),
                                 divf.rearrange("p (a o) -> p a o", o=1).broadcast_to([P, 2 * B, NS]), ALU.is_equal))
            v.tensor_tensor(sel_p, at["iota"].rearrange("p (o n) -> p o n", o=1).broadcast_to([P, 2 * B, P]),
                            modf.rearrange("p (a o) -> p a o", o=1).broadcast_to([P, 2 * B, P]), ALU.is_equal).then_inc(s["sel_ok"], 1)
            for w in range(3):
                ins = v.tensor_tensor(sel_v[:, :, w, :], one_s, vals[:, :, w:w + 1].broadcast_to([P, 2 * B, NS]), ALU.mult)
            ins.then_inc(s["sel_ok"], 1)
            sc, es, prev = tmp(NS, E), tmp(NS), tmp(NS)
            then(v.tensor_tensor(sc, at["iota"][:, 0:NS].rearrange("p (n o) -> p n o", o=1).broadcast_to([P, NS, E]),
                                 last.rearrange("p (o e) -> p o e", o=1).broadcast_to([P, NS, E]), ALU.is_ge))
            then(v.tensor_reduce(es, sc, AX_X, ALU.add))
            esi = tmp(NS).bitcast(I32)
            v.tensor_copy(esi, es)
            v.memset(prev[:, 0:1], 1.0)
            then(v.tensor_tensor(prev[:, 1:NS], es[:, 1:NS], es[:, 0:NS - 1], ALU.subtract))
            flag = tmp(NS)
            then(v.tensor_scalar(flag, es, E - 1.0, None, ALU.is_lt))
            then(v.tensor_tensor(flag, flag, prev, ALU.mult))
            v.tensor_scalar(tab[:, 0, :], esi, 1, None, ALU.bitwise_and)
            v.tensor_scalar(tab[:, 1, :], es, 1.0, None, ALU.add)
            v.tensor_copy(tab[:, 2, :], flag)
            v.tensor_scalar(nslot[:, 0:1], last[:, E - 1:E], -3.0, None, ALU.add)
            par = tmp(NS)
            then(v.memset(hold[:], 0.0))
            then(v.tensor_copy(par, tab[:, 0, :]))
            then(v.tensor_scalar(tab[:, 3, :], par, -1.0, 1.0, ALU.mult, ALU.add))
            dve.wait_ge(s["whi_ok"], 1)
            v.tensor_tensor(wexp[:, 0, 1, :], wraw[:], wexp[:, 0, 0, :].bitcast(F32), ALU.subtract).then_inc(s["wlo_ok"], 1)
            dve.wait_ge(s["inv_ps"], 1)
            inv, pad = tmp(3, NS), tmp(NS)
            then(v.tensor_copy(inv, vp[:, 0:3 * NS].rearrange("p (v n) -> p v n", v=3)))
            v.tensor_tensor(w_sb[:], inv[:, 1], inv[:, 2], ALU.add)
            then(v.tensor_scalar(pad, inv[:, 0], 0.0, at["spare"], ALU.is_equal, ALU.mult))
            then(v.scalar_tensor_tensor(out=ids_sb[:], in0=inv[:, 0], scalar=-1.0, in1=pad, op0=ALU.add, op1=ALU.add))
            v.tensor_copy(idg[:], ids_sb[:, 0:1]).then_inc(s["m_idg"], 1)
            v.memset(hold[:], 0.0).then_inc(s["tab_set"], 1)
            dve.wait_ge(s["tab_set"], 1)

            def moe(k, X, M1, M2):
                if X:
                    dve.wait_ge(s["m_xT"], k + 1)
                    v.tensor_scalar(idg[:], ids_sb[:, bass.ds(k + 1, 1)], 0.0, None, ALU.add).then_inc(s["m_idg"], 1)
                if M2:
                    split_next(dve, k, True)
                    dve.wait_ge(s["m_hhi"], k - 1)
                    v.tensor_tensor(oT_lo[:, 0:KF, :].rearrange("p k n -> p (k n)"), vp[:, 0:KF * P],
                                    oT_hi[:, 0:KF, :].rearrange("p k n -> p (k n)").bitcast(F32), ALU.subtract).then_inc(s["m_hlo"], 1)
                if M1:
                    dve.wait_ge(s["m_silu"], k)
                    wait_prev(dve, s["m_hT"], k - 1)
                    v.tensor_tensor(hsb[:, 0:FH], qk_ps[:, 1, 0:FH], gsb, ALU.mult).then_inc(s["m_h"], 1)
                if X:
                    dve.wait_ge(s["m_xhi"], k + 1)
                    v.tensor_tensor(xnT_lo[:].rearrange("p k n -> p (k n)"), t0[:],
                                    xnT_hi[:].rearrange("p k n -> p (k n)").bitcast(F32), ALU.subtract).then_inc(s["m_xlo"], 1)
                if M2:
                    dve.wait_ge(s["m_y"], k - 1)
                    wait_prev(dve, s["m_sc"], 16 * (k - 2))
                    v.tensor_scalar(ids_out[:], ids_sb[:, bass.ds(k - 2, 1)], 0.0, None, ALU.add)
                    v.tensor_scalar(o_sb[:], tp[:, 0, :], w_sb[:, bass.ds(k - 2, 1)], None, ALU.mult).then_inc(s["m_yok"], 1)
            slots(dve, moe)


def kernel(**inputs):
    import numpy as np
    import concourse.bacc as bacc
    from concourse.bass_utils import run_bass_kernel_spmd

    f32 = np.float32
    T, DM, HW = 128, 512, 32
    a = {n: np.ascontiguousarray(v) for n, v in inputs.items()}
    NB = a["x"].shape[0]
    freqs = (1.0 / f32(10000.0) ** (np.arange(0, HW, 2, dtype=f32) / f32(HW))).astype(f32)
    angle = np.outer(np.arange(T, dtype=f32), freqs).astype(f32)
    sin = np.repeat(np.sin(angle), 2, axis=-1)
    sin[:, 0::2] *= -1
    NE, FF, KB = a["L0_ffn_W1"].shape[0], a["L0_ffn_W1"].shape[1], DM // 128
    moe = np.zeros((NE, 128, 2 * KB * FF + 3 * DM), f32)
    w12 = moe[:, :, :2 * KB * FF].reshape(NE, 128, KB, 2, FF)
    for g, n in enumerate(("L0_ffn_W1", "L0_ffn_W2")):
        w12[:, :, :, g, :] = a[n].reshape(NE, FF, KB, 128).transpose(0, 3, 2, 1)
    w3 = moe[:, :, 2 * KB * FF:].reshape(NE, 128, 3, DM)
    for k in range(3):
        n = min(128, FF - 128 * k)
        w3[:, :n, k, :] = a["L0_ffn_W3"][:, :, 128 * k:128 * k + n].transpose(0, 2, 1)
    row = np.arange(128)
    col = lambda v: np.broadcast_to(np.asarray(v, f32), (128, len(v)))
    consts = {
        "ident": np.eye(128), "cos": np.repeat(np.cos(angle), 2, axis=-1), "sin": sin, "iota": col(row),
        "tri": np.triu(np.ones((128, 128)), 1), "ones": np.ones((128, 128)),
        "mask": col(np.tile(np.arange(NB) > 0, NE)), "thr": col(128 * np.arange(1, NB)),
        "tok": row[:, None] + 1 + 128 * np.tile(np.arange(NB), 2)[None, :], "spare": NB * T + 1 + row[:, None],
    }
    arrays = {
        "x": a["x"].reshape(NB * T, DM),
        "ctxT": np.ascontiguousarray(a["ctx_2048"].reshape(NB, T, KB, 128).transpose(0, 3, 2, 1)),
        "w_qkv": a["L0_attn_w_qkv"], "w_proj": a["L0_attn_w_proj"],
        "wkv_wu": np.ascontiguousarray(np.stack([a["L0_xattn_w"], a["L0_xattn_u"]]).reshape(2, KB, 128).transpose(2, 0, 1)),
        "wgT": np.ascontiguousarray(a["L0_ffn_Wg"].reshape(NE, KB, 128).transpose(2, 1, 0)),
        "w_moe": moe,
        "consts": np.concatenate([consts[n].astype(f32) for n, _ in CONSTS], axis=1),
    }
    nc = bacc.Bacc("TRN2", target_bir_lowering=False, num_devices=1)
    args = [nc.dram_tensor(n, v.shape, mybir.dt.from_np(v.dtype), kind="ExternalInput").ap() for n, v in arrays.items()]
    x3 = nc.dram_tensor("x3n_rows", (NB * T + 128, DM), F32).ap()
    out = nc.dram_tensor("y_out", (NB * T + 128, DM), F32, kind="ExternalOutput").ap()
    decoder(nc, *args, x3, out)
    r = run_bass_kernel_spmd(nc, [arrays], core_ids=[0])
    return r.results[0]["y_out"][:NB * T].reshape(NB, T, DM)
```

```python
from contextlib import ExitStack

import concourse.bass as bass
from concourse import mybir

F32 = mybir.dt.float32
F32R = mybir.dt.float32r
U32 = mybir.dt.uint32
I32 = mybir.dt.int32
ALU = mybir.AluOpType
ACT = mybir.ActivationFunctionType
AX_X = mybir.AxisListType.X

P = 128
D = 512
KD = D // P
H = 16
HD = D // H
HB = P // HD
NEG = -1e38
EPS = 1e-5
E = 8
FH = 352
KF = 3
W12 = KD * 2 * FH
WE = W12 + KF * D
WQ = WE // 4
NS = 40
SCALE = float(HD) ** -0.5

CONSTS = [("ident", P), ("cos", HD), ("sin", HD), ("iota", P), ("tri", P), ("ones", P), ("mask", P),
          ("thr", 15), ("tok", 32), ("spare", 1)]


def wait_prev(eng, sem, n):
    if isinstance(n, int) and n <= 0:
        return
    eng.wait_ge(sem, n)


def decoder(nc, x, ctxT, w_qkv, w_proj, wkv_wu, wgT, w_moe, consts, x3_dram, out):
    B = x.shape[0] // P
    with ExitStack() as ctx:
        def sb(name, shape, dt=F32):
            return ctx.enter_context(nc.sbuf_tensor(name, shape, dt))

        def ps(name, shape):
            return ctx.enter_context(nc.psum_tensor(name, shape, F32))

        def sem(name):
            return ctx.enter_context(nc.semaphore(name))

        t0 = ps("t0", [P, D])
        vp = ps("vp", [P, D])
        qk_ps = ps("qk_ps", [P, 2, D])
        tp = ps("tp", [P, 2, D])
        so = ps("so", [P, 2, D])

        xres = sb("xres", [P, B, D])
        wbig = sb("wbig", [P, 4 * WE], F32R)
        q3 = KD * 3 * D
        wqkv_hi = wbig[:, 0:q3].rearrange("p (k n) -> p k n", k=KD)
        wqkv_lo = wbig[:, q3:2 * q3].rearrange("p (k n) -> p k n", k=KD)
        wproj_hi = wbig[:, 2 * q3:2 * q3 + KD * D].rearrange("p (k n) -> p k n", k=KD)
        wproj_lo = wbig[:, 2 * q3 + KD * D:2 * q3 + 2 * KD * D].rearrange("p (k n) -> p k n", k=KD)
        wexp = wbig[:].rearrange("p (b s n) -> p b s n", b=2, s=2)
        wraw = sb("wraw", [P, WE])
        cst = sb("cst", [P, consts.shape[1]])
        rot = wraw[:, 0:2 * D].rearrange("p (w n) -> p w n", w=2)
        qk = wraw[:, 2 * D:4 * D].rearrange("p (w n) -> p w n", w=2)
        at = {}
        off = 0
        for name, width in CONSTS:
            at[name] = cst[:, off:off + width]
            off += width
        idm = at["ident"]
        cos_sb, sin_sb = at["cos"], at["sin"]
        wg_sb = sb("wg_sb", [P, KD, E])
        sc_all = sb("sc_all", [P, B, E])
        ids_sb = sb("ids_sb", [P, NS + 1], U32)
        w_sb = sb("w_sb", [P, NS])
        tab = sb("tab", [P, 2, NS], I32)
        nslot = sb("nslot", [P, 1], I32)
        idg = sb("idg", [P, 1], U32)
        ids_out = sb("ids_out", [P, 1], U32)
        holdp = sb("holdp", [P, 3])
        phi = sb("phi", [P, 2 * B], F32R)
        wu_in = sb("wu_in", [P, 2, KD])
        mv1 = sb("mv1", [P, B, 2])
        bst = sb("bst", [P, B, 6])
        ln1 = sb("ln1", [P, B])
        rstd1 = sb("rstd1", [P, B])
        xn = sb("xn", [P, D])
        xnT_hi = sb("xnT_hi", [P, KD, P], F32R)
        xnT_lo = sb("xnT_lo", [P, KD, P], F32R)
        vext = sb("vext", [P, H, HD + 1])
        qT = sb("qT", [P, KD, P])
        kblk = sb("kblk", [P, KD, HB, P])
        mx = sb("mx", [P, H])
        nb = sb("nb", [P, H])
        rinv = sb("rinv", [P, H])
        o_sb = sb("o_sb", [P, D])
        oT_hi = sb("oT_hi", [P, KD, P], F32R)
        oT_lo = sb("oT_lo", [P, KD, P], F32R)
        mv2 = sb("mv2", [P, 2])
        bst2 = sb("bst2", [P, 6])
        rstd2 = sb("rstd2", [P, 2])
        kn = sb("kn", [P, D])
        kT = sb("kT", [P, D])
        vT = sb("vT", [P, D])
        wtab = sb("wtab", [P, 2, KD, P])
        omax = sb("omax", [P, 1 + D])
        kk = sb("kk", [P, 2, D])
        pq = sb("pq", [P, 2, 1 + D])
        rden = sb("rden", [P, D])
        yT = sb("yT", [P, D])
        mv3 = sb("mv3", [P, 2])
        bst3 = sb("bst3", [P, 6])
        rstd3 = sb("rstd3", [P, 2])
        eps_c = sb("eps_c", [P, 1])
        hold = sb("hold", [P, 1])
        x3n = sb("x3n", [P, D])
        scratch = sb("scratch", [P, 4 * 2048])
        wqkv_raw = scratch[:, 0:KD * 3 * D].rearrange("p (k n) -> p k n", k=KD)
        wproj_raw = scratch[:, KD * 3 * D:].rearrange("p (k n) -> p k n", k=KD)
        prob = scratch[:, 0:2048].rearrange("p (h n) -> p h n", h=H)
        probT = scratch[:, 2048:4096].rearrange("p (h n) -> p h n", h=H)
        relu = scratch[:, 4096:6144].rearrange("p (s n) -> p s n", s=4)
        ez = scratch[:, 6144:8192].rearrange("p (s n) -> p s n", s=4)
        apq = relu[:, 0:2]
        x3T = relu[:, 2]
        hsb = qT[:].rearrange("p k n -> p (k n)")[:, 0:KF * P]
        gsb = kT[:, 0:FH]
        ea = kk

        names = """const_in w_tab_in wg_in stats1 mean1 lnv1 rstd1_ok xn_ok xnT_ps xhi xlo q_ps k_ps v_ps
        rope_a qk_ok ropeq_read ropek_read v_ok qT_ps kT_ps qT_ok kb_ok zero_ok s_ps
        mx_ok nb_ok exp_ok pt_ps pt_ok pv_ps rinv_ok o_ok oT_ps ohi olo proj_ps x1_ok st2 mv2_ok
        ln2 rs2 kn_ok knT_ps kT_ok vT_in ev_ok tab_ok om_ok kk_ok dm_ok rla rlb ea_ok ez_ok p_ok q_ok ap_ok
        nd_ok lnd rd_ok y_ok yT_ps x2_ok st3 mv3_ok ln3 rs3 x3_ok x3_out wsplit_act wsplit_dve
        whi_ok x2_out spare_out x3T_ps x3T_ok sc_ps sc_ok top_ok oh_ok
        ds_ok e12_ok rk_ps one_ok rows_ok val_ok last_ok inv_ps tab_set step m_idg m_xg m_xT m_xhi m_xlo m_gu m_silu m_h m_hT
        m_hhi m_hlo m_y m_yok m_sc held held_x held_y""".split()
        s = {n: sem(n) for n in names}
        x_in = [sem(f"x_in{g}") for g in range(4)]
        wq_in = [sem(f"wq_in{k}") for k in range(KD)]
        wlo_ok = [sem("wlo_even"), sem("wlo_odd")]
        wv_in = sem("wv_in")
        wp_in = sem("wp_in")
        wraw_in = [sem("wraw_in0"), sem("wraw_in1")]

        groups = [(0, 1), (1, 4), (4, 10), (10, B)]
        block = ctx.enter_context(nc.Block())

        def schedule(eng, body):
            for i in range(5):
                body(i, True, i >= 1, i >= 2, i >= 3, i >= 4)
            with eng.Fori(5, B) as i:
                body(i, True, True, True, True, True)
            for i in range(B, B + 4):
                body(i, False, i < B + 1, i < B + 2, i < B + 3, True)

        def slots(eng, body):
            n = eng.value_load(nslot[0:1, 0:1], min_val=E - 3, max_val=NS - 4) + 3
            for k in range(3):
                body(k, True, k >= 1, k >= 2)
            with eng.Fori(3, n) as k:
                body(k, True, True, True)
            body(n, False, True, True)
            body(n + 1, False, False, True)

        def split_next(eng, k):
            code = eng.value_load(tab[0:1, 1, bass.ds(k - 2, 1)], min_val=8, max_val=8 * E + 7)
            for half in range(2):
                with eng.If((code >> half) & 1 == 1):
                    other = (code >> 2) & 1
                    nxt = code >> 3
                    if eng is nc.scalar:
                        if half == 0:
                            wait_prev(eng, s["m_y"], k - 2)
                        eng.wait_ge(wraw_in[half], 16 * nxt + 16)
                    for q in (2 * half, 2 * half + 1):
                        a = q * WQ
                        hi = wexp[:, bass.ds(other, 1), 0, a:a + WQ].rearrange("p o n -> p (o n)")
                        lo = wexp[:, bass.ds(other, 1), 1, a:a + WQ].rearrange("p o n -> p (o n)")
                        if eng is nc.scalar:
                            nc.scalar.activation(hi, wraw[:, a:a + WQ], ACT.Copy).then_inc(s["whi_ok"], 1)
                        elif q % 2 == (eng is nc.gpsimd):
                            eng.wait_ge(s["whi_ok"], 4 * nxt + q + 1)
                            eng.tensor_tensor(lo, wraw[:, a:a + WQ], hi.bitcast(F32), ALU.subtract).then_inc(wlo_ok[q % 2], 1)

        CH = 8
        sort = wexp[:, 1].rearrange("p s n -> p (s n)")
        sel_p = sort[:, 0:2 * B * P].rearrange("p (a n) -> p a n", n=P)
        sel_v = sort[:, 2 * B * P:2 * B * (P + 3 * NS)].rearrange("p (a v n) -> p a v n", v=3, n=NS)
        pos = [0]

        def tmp(*shape):
            n = 1
            for d in shape:
                n *= d
            a = scratch[:, pos[0]:pos[0] + n]
            pos[0] += n
            if len(shape) == 1:
                return a
            names = "abcd"[:len(shape)]
            return a.rearrange(f"p ({' '.join(names)}) -> p {' '.join(names)}", **dict(zip(names, shape)))

        top8, idx8 = tmp(B, 8), tmp(B, 8).bitcast(U32)
        ds12, e12 = tmp(B), tmp(B)
        idxf, oh = tmp(2, B), tmp(2, B, E)
        picked3 = tmp(B, E)
        picked = picked3.rearrange("p b e -> p (b e)")
        vals = tmp(2 * B, 3)
        divf, one_s = tmp(2 * B), tmp(2 * B, NS)

        NJ = 2 * B // CH

        def values(eng, j, done):
            at_j = slice(j * CH, (j + 1) * CH)
            eng.wait_ge(s["one_ok"], j + 1)
            eng.tensor_tensor(sel_v[:, at_j], one_s[:, at_j].rearrange("p a (o n) -> p a o n", o=1).broadcast_to([P, CH, 3, NS]),
                              vals[:, at_j].rearrange("p a (v o) -> p a v o", o=1).broadcast_to([P, CH, 3, NS]),
                              ALU.mult).then_inc(s[done], 1)

        @block.gpsimd
        def _(pool):
            def rotate(i, A, Bs, U, C, Ds):
                e = i - 4
                if Ds:
                    pool.wait_ge(s["rd_ok"], e + 1)
                    wait_prev(pool, s["yT_ps"], e)
                    nc.gpsimd.tensor_tensor(yT[:], apq[:, 0, :], rden[:], ALU.mult).then_inc(s["y_ok"], 1)
                if A:
                    for w, read in enumerate(("ropeq_read", "ropek_read")):
                        pool.wait_ge(s["rope_a"], 2 * i + w + 1)
                        pool.wait_ge(s[read], 2 * i + 2)
                        nc.gpsimd.tensor_tensor(qk[:, w, :], qk[:, w, :], rot[:, w, :], ALU.add).then_inc(s["qk_ok"], 1)
            for tile in (kblk, omax, pq, o_sb):
                nc.gpsimd.memset(tile[:], 0.0)
            nc.gpsimd.memset(vext[:, :, HD:HD + 1], 1.0).then_inc(s["zero_ok"], 1)
            schedule(pool, rotate)

            for j in range(NJ - 1):
                values(pool, j, "val_ok")

            pool.wait_ge(s["x3_out"], 16 * B)
            pool.wait_ge(s["x2_out"], 16 * B)
            pool.wait_ge(s["spare_out"], 32)
            nc.gpsimd.memset(holdp[:], 0.0).then_inc(s["held"], 1)
            pool.wait_ge(s["held"], 1)

            def gather():
                nc.gpsimd.indirect_dma_start(xn[:], None, x3_dram, bass.IndirectOffsetOnAxis(ap=idg[:], axis=0)).then_inc(s["m_xg"], 16)

            pool.wait_ge(s["m_idg"], 1)
            gather()

            def carry(c, sem):
                nc.gpsimd.tensor_tensor(holdp[:, c:c + 1], holdp[:, 2:3], holdp[:, 2:3], ALU.add).then_inc(sem, 1)

            def scatter(j):
                wait_prev(pool, s["held_y"], j)
                pool.wait_ge(s["m_yok"], j + 1)
                carry(1, s["held_y"])
                nc.gpsimd.indirect_dma_start(out, bass.IndirectOffsetOnAxis(ap=ids_out[:], axis=0), o_sb[:], None,
                                             compute_op=ALU.add).then_inc(s["m_sc"], 16)

            def moe(k, X, M1, M2):
                if X:
                    wait_prev(pool, s["held_x"], k)
                    pool.wait_ge(s["m_idg"], k + 2)
                    pool.wait_ge(s["m_xT"], k + 1)
                    carry(0, s["held_x"])
                    gather()
                if M2 and not (isinstance(k, int) and k < 3):
                    scatter(k - 3)
                if M2:
                    split_next(nc.gpsimd, k)
            pool.wait_ge(s["tab_set"], 1)
            slots(pool, moe)
            n = pool.value_load(nslot[0:1, 0:1], min_val=E - 3, max_val=NS - 4) + 3
            scatter(n - 1)
            pool.wait_ge(s["m_sc"], 16 * n)
            pool.wait_ge(s["m_xg"], 16 * (n + 1))

        @block.sync
        def _(sp):
            sp.dma_start(cst[:], consts).then_inc(s["const_in"], 16)
            xv = x.rearrange("(b t) d -> t b d", t=P)
            sp.dma_start(xres[:, 0:1, :], xv[:, 0:1, :]).then_inc(x_in[0], 16)
            for k in range(KD):
                sp.dma_start(wqkv_raw[:, k, 0:2 * D], w_qkv[k * P:(k + 1) * P, 0:2 * D]).then_inc(wq_in[k], 16)
            sp.dma_start(wqkv_raw[:, :, 2 * D:], w_qkv[:, 2 * D:].rearrange("(k p) n -> p k n", p=P)).then_inc(wv_in, 16)
            sp.dma_start(wproj_raw, w_proj.rearrange("(k p) n -> p k n", p=P)).then_inc(wp_in, 16)
            sp.dma_start(wg_sb[:], wgT).then_inc(s["wg_in"], 16)
            sp.dma_start(wu_in[:], wkv_wu).then_inc(s["w_tab_in"], 16)
            for g, (a, b) in enumerate(groups[1:]):
                sp.dma_start(xres[:, a:b, :], xv[:, a:b, :]).then_inc(x_in[g + 1], 16)
            sp.wait_ge(s["zero_ok"], 1)
            sp.dma_start(x3_dram[B * P:B * P + P, :], o_sb[:]).then_inc(s["spare_out"], 16)
            sp.dma_start(out[B * P:B * P + P, :], o_sb[:]).then_inc(s["spare_out"], 16)

            def load_expert(e):
                for half in range(2):
                    if e > 0:
                        sp.wait_ge(wlo_ok[0], 2 * (e - 1) + half + 1)
                        sp.wait_ge(wlo_ok[1], 2 * (e - 1) + half + 1)
                    a = 2 * half * WQ
                    sp.dma_start(wraw[:, a:a + 2 * WQ], w_moe[e][:, a:a + 2 * WQ]).then_inc(wraw_in[half], 16)

            def body(i, A, Bs, U, C, Ds):
                if C:
                    c = i - 3
                    wait_prev(sp, s["ev_ok"], c)
                    sp.dma_start(vT[:].rearrange("p (k t) -> p k t", k=KD), ctxT[bass.ds(c, 1)].rearrange("o p k t -> p (o k) t")).then_inc(s["vT_in"], 16)
                if isinstance(i, int) and i == B:
                    sp.wait_ge(s["kT_ps"], B)
                    load_expert(0)
                if Ds:
                    e = i - 4
                    sp.wait_ge(s["x2_ok"], e + 1)
                    sp.dma_start(out[bass.ds(e * P, P), :], xres[:, bass.ds(e, 1), :].rearrange("p o n -> p (o n)")).then_inc(s["x2_out"], 16)
                    sp.wait_ge(s["x3_ok"], e + 1)
                    sp.dma_start(x3_dram[bass.ds(e * P, P), :], x3n[:]).then_inc(s["x3_out"], 16)
            schedule(sp, body)
            for e in range(1, E):
                load_expert(e)
            sp.wait_ge(s["x2_out"], 16 * B)
            sp.wait_ge(s["x3_out"], 16 * B)

        @block.tensor
        def _(pe):
            def three(dst, k, hi, lo, w_hi, w_lo, first, last):
                pe.matmul(dst, hi[:, k, :], w_hi, start=first, stop=False)
                pe.matmul(dst, hi[:, k, :], w_lo, start=False, stop=False)
                return pe.matmul(dst, lo[:, k, :], w_hi, start=False, stop=last)

            def turn(dst, src):
                for k in range(KD):
                    mm = pe.transpose(dst[:, k * P:(k + 1) * P], src[:, k * P:(k + 1) * P], idm)
                return mm

            def project(dst, hi, lo, w_hi, w_lo, a):
                for k in range(KD):
                    mm = three(dst, k, hi, lo, w_hi[:, k, a:a + D], w_lo[:, k, a:a + D], k == 0, k == KD - 1)
                return mm

            pe.wait_ge(s["const_in"], 16)

            def body(i, A, Bs, U, C, Ds):
                t, u, c, e = i - 1, i - 2, i - 3, i - 4

                def score(j):
                    pe.matmul(so[:, j % 2, :], qT[:, j, :], kblk[:, j].rearrange("p r n -> p (r n)"),
                              start=True, stop=True).then_inc(s["s_ps"], 1)

                def turn_prob(j):
                    pe.wait_ge(s["exp_ok"], 4 * t + j + 1)
                    for r in range(HB):
                        mm = pe.transpose(tp[:, j % 2, r * P:(r + 1) * P], prob[:, HB * j + r, :], idm)
                    mm.then_inc(s["pt_ps"], 1)

                def pv(j):
                    for r in range(HB):
                        h = HB * j + r
                        a = (h % 8) * (HD + 1)
                        mm = pe.matmul(so[:, h // 8, a:a + HD + 1], probT[:, h, :], vext[:, h, :], start=True, stop=True)
                    mm.then_inc(s["pv_ps"], 1)

                def turn_kn(c):
                    pe.wait_ge(s["kn_ok"], c + 1)
                    if isinstance(i, int) and i > B:
                        pe.wait_ge(s["pt_ok"], 4 * B)
                        pe.wait_ge(s["kT_ok"], c)
                        turn(tp[:, 0, :], kn).then_inc(s["knT_ps"], 1)
                    else:
                        if isinstance(i, int) and i <= 4:
                            pe.wait_ge(s["xlo"], i)
                        else:
                            pe.wait_ge(s["sc_ok"], e)
                        turn(t0[:], kn).then_inc(s["knT_ps"], 1)

                last = isinstance(i, int) and i == B + 1
                if last:
                    pe.wait_ge(s["o_ok"], 2 * u + 2)
                    pe.wait_ge(s["x1_ok"], u)
                    turn(vp[:], o_sb).then_inc(s["oT_ps"], 1)
                if C and not (isinstance(i, int) and i == B + 2):
                    turn_kn(c)
                if Bs:
                    pe.wait_ge(s["qk_ok"], 2 * t + 2)
                    wait_prev(pe, s["pt_ok"], 4 * t)
                    turn(tp[:, 0, :], qk[:, 0, :]).then_inc(s["qT_ps"], 1)
                    turn(tp[:, 1, :], qk[:, 1, :]).then_inc(s["kT_ps"], 1)
                if Bs:
                    if isinstance(i, int) and i <= 2:
                        wait_prev(pe, s["v_ok"], t)
                    else:
                        pe.wait_ge(s["x1_ok"], i - 2)
                    if isinstance(i, int) and i == 1:
                        pe.wait_ge(s["wsplit_dve"], KD + 1)
                    project(vp[:], xnT_hi, xnT_lo, wqkv_hi, wqkv_lo, 2 * D).then_inc(s["v_ps"], 1)
                if A:
                    pe.wait_ge(s["xn_ok"], i + 1)
                    if C:
                        pe.wait_ge(s["kT_ok"], c + 1)
                    else:
                        wait_prev(pe, s["xlo"], i)
                    turn(t0[:], xn).then_inc(s["xnT_ps"], 1)
                if Bs:
                    pe.wait_ge(s["qT_ok"], t + 1)
                    pe.wait_ge(s["kb_ok"], 4 * t + 4)
                    wait_prev(pe, s["o_ok"], 2 * t)
                    score(0)
                    score(1)
                if U and not last:
                    pe.wait_ge(s["o_ok"], 2 * u + 2)
                    pe.wait_ge(s["v_ok"], t + 1)
                    turn(vp[:], o_sb).then_inc(s["oT_ps"], 1)
                if A:
                    pe.wait_ge(s["xhi"], i + 1)
                    pe.wait_ge(s["xlo"], i + 1)
                    wait_prev(pe, s["ropeq_read"], 2 * i)
                    for k in range(KD):
                        if isinstance(i, int) and i == 0:
                            pe.wait_ge(s["wsplit_dve"], k + 1)
                        mm = three(qk_ps[:, 0, :], k, xnT_hi, xnT_lo, wqkv_hi[:, k, 0:D], wqkv_lo[:, k, 0:D],
                                   k == 0, k == KD - 1)
                    mm.then_inc(s["q_ps"], 1)
                if Bs:
                    pe.wait_ge(s["exp_ok"], 4 * t + 1)
                    score(2)
                    turn_prob(0)
                    pe.wait_ge(s["exp_ok"], 4 * t + 2)
                    score(3)
                    turn_prob(1)
                if Ds:
                    pe.wait_ge(s["y_ok"], e + 1)
                    if A:
                        pe.wait_ge(s["xlo"], i + 1)
                    elif Bs:
                        pe.wait_ge(s["kT_ok"], c + 1)
                    else:
                        pe.wait_ge(s["sc_ok"], e)
                    turn(t0[:], yT).then_inc(s["yT_ps"], 1)
                if U:
                    if isinstance(i, int) and i == 2:
                        pe.wait_ge(s["wsplit_dve"], KD + 2)
                    pe.wait_ge(s["ohi"], u + 1)
                    pe.wait_ge(s["olo"], u + 1)
                    project(vp[:], oT_hi, oT_lo, wproj_hi, wproj_lo, 0).then_inc(s["proj_ps"], 1)
                if last:
                    turn_kn(B - 1)
                if A:
                    wait_prev(pe, s["ropek_read"], 2 * i)
                for k in range(KD):
                    if A:
                        mm = three(qk_ps[:, 1, :], k, xnT_hi, xnT_lo, wqkv_hi[:, k, D:2 * D], wqkv_lo[:, k, D:2 * D],
                                   k == 0, k == KD - 1)
                        if k == KD - 1:
                            mm.then_inc(s["k_ps"], 1)
                    if Bs and k < 2:
                        if k == 0:
                            pe.wait_ge(s["exp_ok"], 4 * t + 3)
                        pe.wait_ge(s["pt_ok"], 4 * t + k + 1)
                        pv(k)
                if Bs:
                    pe.wait_ge(s["pt_ok"], 4 * t + 1)
                    turn_prob(2)
                    pe.wait_ge(s["pt_ok"], 4 * t + 2)
                    turn_prob(3)
                if Ds:
                    pe.wait_ge(s["x3_ok"], e + 1)
                    turn(t0[:], x3n).then_inc(s["x3T_ps"], 1)
                if Bs:
                    pe.wait_ge(s["pt_ok"], 4 * t + 3)
                    pv(2)
                if Ds:
                    if isinstance(i, int) and i == 4:
                        pe.wait_ge(s["wg_in"], 16)
                    pe.wait_ge(s["x3T_ok"], e + 1)
                    for k in range(KD):
                        mm = pe.matmul(t0[:, 0:E], x3T[:, k * P:(k + 1) * P], wg_sb[:, k, :], start=k == 0, stop=k == KD - 1)
                    mm.then_inc(s["sc_ps"], 1)
                if Bs:
                    pe.wait_ge(s["pt_ok"], 4 * t + 4)
                    pv(3)
            schedule(pe, body)

            pe.wait_ge(s["oh_ok"], 3)
            pe.matmul(t0[:, 0:P], at["tri"], picked, start=True, stop=True)
            pe.matmul(t0[:, P:2 * P], at["ones"], picked, start=True, stop=True).then_inc(s["rk_ps"], 1)
            for a in range(2 * B):
                if a % CH == 0:
                    pe.wait_ge(s["rows_ok"], a // CH + 1)
                    if a // CH < NJ - 1:
                        pe.wait_ge(s["val_ok"], a // CH + 1)
                    else:
                        pe.wait_ge(s["last_ok"], 1)
                mm = pe.matmul(vp[:, 0:3 * NS], sel_p[:, a, :], sel_v[:, a].rearrange("p v n -> p (v n)"),
                               start=a == 0, stop=a == 2 * B - 1)
            mm.then_inc(s["inv_ps"], 1)

            pe.wait_ge(s["tab_set"], 1)

            def moe(k, X, M1, M2):
                if M1 or M2:
                    code = pe.value_load(tab[0:1, 0, bass.ds(k - 1, 1)], min_val=2, max_val=2 * E + 3)
                    par2 = code & 1
                    need = code >> 1
                    par1 = (need + 1) & 1
                if M2:
                    pe.wait_ge(s["m_h"], k - 1)
                    wait_prev(pe, s["m_hlo"], k - 2)
                    for f in range(KF):
                        n = min(P, FH - f * P)
                        mm = pe.transpose(vp[0:n, f * P:(f + 1) * P], hsb[:, f * P:f * P + n], idm)
                    mm.then_inc(s["m_hT"], 1)
                if X:
                    pe.wait_ge(s["m_xg"], 16 * (k + 1))
                    wait_prev(pe, s["m_xlo"], k)
                    turn(t0[:], xn).then_inc(s["m_xT"], 1)
                if M1:
                    pe.wait_ge(wlo_ok[0], 2 * need)
                    pe.wait_ge(wlo_ok[1], 2 * need)
                    pe.wait_ge(s["m_xlo"], k)
                    wait_prev(pe, s["m_h"], k - 1)
                    for g in range(2):
                        for f in range(KD):
                            a = f * 2 * FH + g * FH
                            w_hi = wexp[:, bass.ds(par1, 1), 0, a:a + FH].rearrange("p o n -> p (o n)")
                            w_lo = wexp[:, bass.ds(par1, 1), 1, a:a + FH].rearrange("p o n -> p (o n)")
                            mm = three(qk_ps[:, g, 0:FH], f, xnT_hi, xnT_lo, w_hi, w_lo, f == 0, f == KD - 1)
                    mm.then_inc(s["m_gu"], 1)
                if M2:
                    pe.wait_ge(s["m_hlo"], k - 1)
                    wait_prev(pe, s["m_yok"], k - 2)
                    for f in range(KF):
                        n = min(P, FH - f * P)
                        a = W12 + f * D
                        w_hi = wexp[0:n, bass.ds(par2, 1), 0, a:a + D].rearrange("p o n -> p (o n)")
                        w_lo = wexp[0:n, bass.ds(par2, 1), 1, a:a + D].rearrange("p o n -> p (o n)")
                        mm = three(tp[:, 0, :], f, oT_hi[0:n], oT_lo[0:n], w_hi, w_lo, f == 0, f == KF - 1)
                    mm.then_inc(s["m_y"], 1)
            slots(pe, moe)

        @block.scalar
        def _(act):
            nc.scalar.preload_act_table_set("natural_log_exp_and_others")
            def rstd(g):
                a, b = groups[g]
                act.wait_ge(s["mean1"], b)
                nc.scalar.activation(ln1[:, a:b], mv1[:, a:b, 1], ACT.Ln, bias=eps_c[:, 0:1]).then_inc(s["lnv1"], 1)
                act.wait_ge(s["lnv1"], g + 1)
                nc.scalar.activation(rstd1[:, a:b], ln1[:, a:b], ACT.Exp, scale=-0.5).then_inc(s["rstd1_ok"], 1)

            rstd(0)

            def body(i, A, Bs, U, C, Ds):
                t, u, c, e = i - 1, i - 2, i - 3, i - 4

                def exps(j):
                    act.wait_ge(s["nb_ok"], 4 * t + j + 1)
                    wait_prev(act, s["pt_ps"], 4 * t + j - 3 if not isinstance(t, int) or t > 0 else 0)
                    for r in range(HB):
                        h = HB * j + r
                        a = nc.scalar.activation(prob[:, h, :], so[:, j % 2, r * P:(r + 1) * P], ACT.Exp,
                                                 bias=nb[:, h:h + 1], scale=SCALE)
                    a.then_inc(s["exp_ok"], 1)

                def take_prob(j):
                    act.wait_ge(s["pt_ps"], 4 * t + j + 1)
                    wait_prev(act, s["pv_ps"], 4 * t if not isinstance(t, int) or t > 0 else 0)
                    nc.scalar.activation(probT[:, HB * j:HB * j + HB, :].rearrange("p h n -> p (h n)"),
                                         tp[:, j % 2, :], ACT.Copy).then_inc(s["pt_ok"], 1)

                def take_kT(c):
                    act.wait_ge(s["knT_ps"], c + 1)
                    wait_prev(act, s["kk_ok"], c)
                    nc.scalar.activation(kT[:], tp[:, 0, :] if isinstance(i, int) and i > B else t0[:],
                                         ACT.Copy).then_inc(s["kT_ok"], 1)

                def take_o():
                    act.wait_ge(s["oT_ps"], u + 1)
                    wait_prev(act, s["proj_ps"], u)
                    nc.scalar.activation(oT_hi[:].rearrange("p k n -> p (k n)"), vp[:], ACT.Copy).then_inc(s["ohi"], 1)

                if C and not (isinstance(i, int) and i == B + 2):
                    take_kT(c)
                if U and not Bs:
                    take_o()
                    for q in range(4):
                        if q % 2 == 0:
                            act.wait_ge(wraw_in[q // 2], 16)
                        nc.scalar.activation(wexp[:, 0, 0, q * WQ:(q + 1) * WQ], wraw[:, q * WQ:(q + 1) * WQ],
                                             ACT.Copy).then_inc(s["whi_ok"], 1)
                if Bs:
                    act.wait_ge(s["kT_ps"], t + 1)
                    if isinstance(i, int) and i == 1:
                        act.wait_ge(s["zero_ok"], 1)
                    for r in range(HB):
                        nc.scalar.activation(kblk[HD * r:HD * r + HD, :, r, :],
                                             tp[HD * r:HD * r + HD, 1, :].rearrange("p (k n) -> p k n", k=KD),
                                             ACT.Copy).then_inc(s["kb_ok"], 1)
                if Bs:
                    act.wait_ge(s["v_ps"], t + 1)
                    wait_prev(act, s["pv_ps"], 4 * t)
                    nc.scalar.activation(vext[:, :, 0:HD], vp[:].rearrange("p (h d) -> p h d", h=H),
                                         ACT.Copy).then_inc(s["v_ok"], 1)
                if A:
                    act.wait_ge(s["xnT_ps"], i + 1)
                    wait_prev(act, s["v_ps"], i)
                    nc.scalar.activation(xnT_hi[:].rearrange("p k n -> p (k n)"), t0[:], ACT.Copy).then_inc(s["xhi"], 1)
                if isinstance(i, int) and i == 0:
                    for k in range(KD):
                        act.wait_ge(wq_in[k], 16)
                        nc.scalar.activation(wqkv_hi[:, k, 0:2 * D], wqkv_raw[:, k, 0:2 * D], ACT.Copy).then_inc(s["wsplit_act"], 1)
                    act.wait_ge(wv_in, 16)
                    nc.scalar.activation(wqkv_hi[:, :, 2 * D:], wqkv_raw[:, :, 2 * D:], ACT.Copy).then_inc(s["wsplit_act"], 1)
                    act.wait_ge(wp_in, 16)
                    nc.scalar.activation(wproj_hi, wproj_raw, ACT.Copy).then_inc(s["wsplit_act"], 1)
                if C:
                    act.wait_ge(s["dm_ok"], c + 1)
                    wait_prev(act, s["sc_ps"], c - 1)
                    nc.scalar.activation(relu[:, 2:4, :], kk[:], ACT.Relu).then_inc(s["rlb"], 1)
                if Bs:
                    exps(0)
                if Bs:
                    exps(1)
                if U and Bs:
                    take_o()
                if Bs:
                    take_prob(0)
                if Bs:
                    take_prob(1)
                if C:
                    act.wait_ge(s["rlb"], c + 1)
                    wait_prev(act, s["nd_ok"], c)
                    nc.scalar.activation(ez[:].rearrange("p (a b) n -> p a b n", b=2)[:, :, 1, :], relu[:, 2:4, :],
                                         ACT.Exp, scale=-1.0).then_inc(s["ez_ok"], 1)
                if Bs:
                    exps(2)
                if C:
                    wait_prev(act, s["y_ok"], c)
                    nc.scalar.activation(relu[:, 0:2, :], kk[:], ACT.Relu, scale=-1.0).then_inc(s["rla"], 1)
                if C:
                    act.wait_ge(s["rla"], c + 1)
                    nc.scalar.activation(ea[:], relu[:, 0:2, :], ACT.Exp, scale=-1.0).then_inc(s["ea_ok"], 1)
                if Bs:
                    exps(3)
                if Ds:
                    act.wait_ge(s["mv3_ok"], e + 1)
                    nc.scalar.activation(rstd3[:, 0:1], mv3[:, 1:2], ACT.Ln, bias=eps_c[:, 0:1]).then_inc(s["ln3"], 1)
                    act.wait_ge(s["ln3"], e + 1)
                    nc.scalar.activation(rstd3[:, 1:2], rstd3[:, 0:1], ACT.Exp, scale=-0.5).then_inc(s["rs3"], 1)
                if U:
                    act.wait_ge(s["mv2_ok"], u + 1)
                    nc.scalar.activation(rstd2[:, 0:1], mv2[:, 1:2], ACT.Ln, bias=eps_c[:, 0:1]).then_inc(s["ln2"], 1)
                    act.wait_ge(s["ln2"], u + 1)
                    nc.scalar.activation(rstd2[:, 1:2], rstd2[:, 0:1], ACT.Exp, scale=-0.5).then_inc(s["rs2"], 1)
                if Bs:
                    take_prob(2)
                if Bs:
                    take_prob(3)
                if isinstance(i, int) and i == B + 1:
                    take_kT(B - 1)
                if Ds:
                    act.wait_ge(s["x3T_ps"], e + 1)
                    wait_prev(act, s["sc_ps"], e)
                    if C:
                        act.wait_ge(s["ez_ok"], c + 1)
                    nc.scalar.activation(x3T, t0[:], ACT.Copy).then_inc(s["x3T_ok"], 1)
                if C:
                    act.wait_ge(s["nd_ok"], c + 1)
                    wait_prev(act, s["y_ok"], c)
                    nc.scalar.activation(rden[:], apq[:, 1, :], ACT.Ln).then_inc(s["lnd"], 1)
                    act.wait_ge(s["lnd"], c + 1)
                    nc.scalar.activation(rden[:], rden[:], ACT.Exp, scale=-1.0).then_inc(s["rd_ok"], 1)
                if isinstance(i, int) and i < len(groups) - 1:
                    rstd(i + 1)
            schedule(act, body)

            act.wait_ge(s["ds_ok"], 1)
            nc.scalar.activation(e12, ds12, ACT.Exp).then_inc(s["e12_ok"], 1)
            act.wait_ge(s["tab_set"], 1)

            def moe(k, X, M1, M2):
                if M2:
                    act.wait_ge(s["m_hT"], k - 1)
                    wait_prev(act, s["m_y"], k - 2)
                    nc.scalar.activation(oT_hi[:, 0:KF, :].rearrange("p k n -> p (k n)"), vp[:, 0:KF * P],
                                         ACT.Copy).then_inc(s["m_hhi"], 1)
                    split_next(nc.scalar, k)
                if M1:
                    act.wait_ge(s["m_gu"], k)
                    wait_prev(act, s["m_h"], k - 1)
                    nc.scalar.activation(gsb, qk_ps[:, 0, 0:FH], ACT.Silu).then_inc(s["m_silu"], 1)
                if X:
                    act.wait_ge(s["m_xT"], k + 1)
                    wait_prev(act, s["m_gu"], k)
                    nc.scalar.activation(xnT_hi[:].rearrange("p k n -> p (k n)"), t0[:], ACT.Copy).then_inc(s["m_xhi"], 1)
            slots(act, moe)

        @block.vector
        def _(dve):
            v = nc.vector
            v.memset(eps_c[:], EPS)

            def stats(g):
                dve.wait_ge(x_in[g], 16)
                for b in range(*groups[g]):
                    v.bn_stats(bst[:, b, :], xres[:, b, :]).then_inc(s["stats1"], 1)
                for b in range(*groups[g]):
                    dve.wait_ge(s["stats1"], b + 1)
                    v.bn_aggr(mv1[:, b, :], bst[:, b, :]).then_inc(s["mean1"], 1)

            def rest(n, lo, raw, hi):
                dve.wait_ge(s["wsplit_act"], n)
                v.tensor_tensor(lo, raw, hi.bitcast(F32), ALU.subtract).then_inc(s["wsplit_dve"], 1)

            stats(0)
            dve.wait_ge(s["zero_ok"], 1)

            def normalise(dst, src, mean, rstd):
                return v.tensor_scalar(dst, src, mean, rstd, ALU.subtract, ALU.mult)

            def top(a, b):
                dve.wait_ge(s["sc_ok"], b)
                for tile in range(a, b):
                    v.max(top8[:, tile, :], sc_all[:, tile, :]).then_inc(s["top_ok"], 1)
                for tile in range(a, b):
                    dve.wait_ge(s["top_ok"], tile + 1)
                    v.max_index(idx8[:, tile, :], top8[:, tile, :], sc_all[:, tile, :]).then_inc(s["step"], 1)

            def body(i, A, Bs, U, C, Ds):
                t, u, c, e = i - 1, i - 2, i - 3, i - 4

                def maxes(j):
                    dve.wait_ge(s["s_ps"], 4 * t + j + 1)
                    v.tensor_reduce(mx[:, HB * j:HB * j + HB], so[:, j % 2, :].rearrange("p (r n) -> p r n", r=HB),
                                    AX_X, ALU.max).then_inc(s["mx_ok"], 1)
                    dve.wait_ge(s["mx_ok"], 4 * t + j + 1)
                    v.tensor_scalar(nb[:, HB * j:HB * j + HB], mx[:, HB * j:HB * j + HB], -SCALE, None,
                                    ALU.mult).then_inc(s["nb_ok"], 1)

                def rope(w, ready, read):
                    dve.wait_ge(s[ready], i + 1)
                    wait_prev(dve, s["qk_ok"], 2 * i)
                    src = qk_ps[:, w, :].rearrange("p (h d) -> p h d", h=H)
                    cosb = cos_sb.rearrange("p (o d) -> p o d", o=1).broadcast_to([P, H, HD])
                    v.tensor_tensor(rot[:, w, :].rearrange("p (h d) -> p h d", h=H), src, cosb,
                                    ALU.mult).then_inc(s["rope_a"], 1)
                    s4 = qk_ps[:, w, :].rearrange("p (h d two) -> p h d two", h=H, two=2)
                    d4 = qk[:, w, :].rearrange("p (h d two) -> p h d two", h=H, two=2)
                    for a in range(2):
                        sn = sin_sb.rearrange("p (o d two) -> p o d two", o=1, two=2)[:, :, :, a].broadcast_to([P, H, HD // 2])
                        v.tensor_tensor(d4[:, :, :, a], s4[:, :, :, 1 - a], sn, ALU.mult).then_inc(s[read], 1)

                if A:
                    if isinstance(i, int):
                        dve.wait_ge(s["rstd1_ok"], sum(i >= a for a, b in groups))
                    elif A:
                        dve.wait_ge(s["rstd1_ok"], len(groups))
                    wait_prev(dve, s["xnT_ps"], i)
                    normalise(xn[:], xres[:, bass.ds(i, 1), :].rearrange("p o n -> p (o n)"), mv1[:, bass.ds(i, 1), 0], rstd1[:, bass.ds(i, 1)]).then_inc(s["xn_ok"], 1)
                if Bs:
                    dve.wait_ge(s["qT_ps"], t + 1)
                    v.tensor_copy(qT[:].rearrange("p k n -> p (k n)"), tp[:, 0, :]).then_inc(s["qT_ok"], 1)
                def rest_o():
                    dve.wait_ge(s["ohi"], u + 1)
                    v.tensor_tensor(oT_lo[:].rearrange("p k n -> p (k n)"), vp[:],
                                    oT_hi[:].rearrange("p k n -> p (k n)").bitcast(F32), ALU.subtract).then_inc(s["olo"], 1)

                if U and not Bs:
                    rest_o()
                if C:
                    dve.wait_ge(s["kT_ok"], c + 1)
                    v.tensor_tensor_scan(omax[:, 1:], wtab[:, 0].rearrange("p k n -> p (k n)"), kT[:], 0.0, ALU.add, ALU.max).then_inc(s["om_ok"], 1)
                    v.tensor_tensor(kk[:], kT[:].rearrange("p (o n) -> p o n", o=1).broadcast_to([P, 2, D]),
                                    wtab[:].rearrange("p a k n -> p a (k n)"), ALU.subtract).then_inc(s["kk_ok"], 1)
                    dve.wait_ge(s["om_ok"], c + 1)
                    dve.wait_ge(s["kk_ok"], c + 1)
                    v.tensor_tensor(kk[:], omax[:, 0:D].rearrange("p (o n) -> p o n", o=1).broadcast_to([P, 2, D]),
                                    kk[:], ALU.subtract).then_inc(s["dm_ok"], 1)
                if isinstance(i, int) and i == 1:
                    stats(2)
                if isinstance(i, int) and i == 2:
                    dve.wait_ge(s["w_tab_in"], 16)
                    v.tensor_copy(wtab[:, 0], wu_in[:, 0, :].rearrange("p (k o) -> p k o", o=1).broadcast_to([P, KD, P])).then_inc(s["tab_ok"], 1)
                    v.tensor_scalar(wtab[:, 1], wu_in[:, 1, :].rearrange("p (k o) -> p k o", o=1).broadcast_to([P, KD, P]),
                                    -1.0, None, ALU.mult).then_inc(s["tab_ok"], 1)
                    dve.wait_ge(s["tab_ok"], 2)
                    v.memset(wtab[:, :, :, 0:1], NEG).then_inc(s["tab_ok"], 1)
                    dve.wait_ge(s["tab_ok"], 3)
                    stats(3)
                def first_rest(quarters):
                    for q in quarters:
                        dve.wait_ge(s["whi_ok"], q + 1)
                        v.tensor_tensor(wexp[:, 0, 1, q * WQ:(q + 1) * WQ], wraw[:, q * WQ:(q + 1) * WQ],
                                        wexp[:, 0, 0, q * WQ:(q + 1) * WQ].bitcast(F32), ALU.subtract).then_inc(wlo_ok[q % 2], 1)

                def take_scores(e):
                    dve.wait_ge(s["sc_ps"], e + 1)
                    v.tensor_scalar(sc_all[:, bass.ds(e, 1), :].rearrange("p o n -> p (o n)"), t0[:, 0:E], 0.0, None,
                                    ALU.add).then_inc(s["sc_ok"], 1)

                if isinstance(i, int) and i == B + 2:
                    take_scores(e - 1)
                    first_rest((0,))
                if isinstance(i, int) and i == B + 3:
                    first_rest((1, 2))
                if A:
                    dve.wait_ge(s["xhi"], i + 1)
                    v.tensor_tensor(xnT_lo[:].rearrange("p k n -> p (k n)"), t0[:],
                                    xnT_hi[:].rearrange("p k n -> p (k n)").bitcast(F32), ALU.subtract).then_inc(s["xlo"], 1)
                if isinstance(i, int) and i == 0:
                    for k in range(KD):
                        rest(k + 1, wqkv_lo[:, k, 0:2 * D], wqkv_raw[:, k, 0:2 * D], wqkv_hi[:, k, 0:2 * D])
                if Bs:
                    maxes(0)
                    maxes(1)
                if A:
                    rope(0, "q_ps", "ropeq_read")
                if U and Bs:
                    rest_o()
                if Bs:
                    maxes(2)
                    maxes(3)
                if isinstance(i, int) and i == 1:
                    rest(KD + 2, wproj_lo, wproj_raw, wproj_hi)
                if Ds:
                    xr = xres[:, bass.ds(e, 1), :].rearrange("p o n -> p (o n)")
                    dve.wait_ge(s["yT_ps"], e + 1)
                    v.tensor_tensor(xr, xr, t0[:], ALU.add).then_inc(s["x2_ok"], 1)
                    dve.wait_ge(s["x2_ok"], e + 1)
                    v.memset(hold[:], 0.0)
                    v.bn_stats(bst3[:], xr).then_inc(s["st3"], 1)
                    dve.wait_ge(s["st3"], e + 1)
                    v.memset(hold[:], 0.0)
                    v.bn_aggr(mv3[:], bst3[:]).then_inc(s["mv3_ok"], 1)
                if C:
                    ez4 = ez[:].rearrange("p (a b) n -> p a b n", b=2)
                    dve.wait_ge(s["ez_ok"], c + 1)
                    dve.wait_ge(s["vT_in"], 16 * (c + 1))
                    v.tensor_tensor(ez4[:, :, 0, :], ez4[:, :, 1, :],
                                    vT[:].rearrange("p (o n) -> p o n", o=1).broadcast_to([P, 2, D]), ALU.mult).then_inc(s["ev_ok"], 1)
                if U:
                    xu = xres[:, bass.ds(u, 1), :].rearrange("p o n -> p (o n)")
                    dve.wait_ge(s["proj_ps"], u + 1)
                    v.tensor_tensor(xu, xu, vp[:], ALU.add).then_inc(s["x1_ok"], 1)
                    dve.wait_ge(s["x1_ok"], u + 1)
                    v.memset(hold[:], 0.0)
                    v.bn_stats(bst2[:], xu).then_inc(s["st2"], 1)
                    dve.wait_ge(s["st2"], u + 1)
                    v.memset(hold[:], 0.0)
                    v.bn_aggr(mv2[:], bst2[:]).then_inc(s["mv2_ok"], 1)
                if C:
                    dve.wait_ge(s["ea_ok"], c + 1)
                    v.tensor_tensor_scan(pq[:, 1, 1:], ea[:, 0, :], ez[:, 1, :], 0.0, ALU.mult, ALU.add).then_inc(s["q_ok"], 1)
                if Ds:
                    dve.wait_ge(s["rs3"], e + 1)
                    wait_prev(dve, s["x3_out"], 16 * e)
                    normalise(x3n[:], xr, mv3[:, 0:1], rstd3[:, 1:2]).then_inc(s["x3_ok"], 1)
                if C:
                    dve.wait_ge(s["ev_ok"], c + 1)
                    v.tensor_tensor_scan(pq[:, 0, 1:], ea[:, 0, :], ez[:, 0, :], 0.0, ALU.mult, ALU.add).then_inc(s["p_ok"], 1)
                if U:
                    dve.wait_ge(s["rs2"], u + 1)
                    wait_prev(dve, s["knT_ps"], u)
                    normalise(kn[:], xu, mv2[:, 0:1], rstd2[:, 1:2]).then_inc(s["kn_ok"], 1)
                if isinstance(i, int) and i == 0:
                    rest(KD + 1, wqkv_lo[:, :, 2 * D:], wqkv_raw[:, :, 2 * D:], wqkv_hi[:, :, 2 * D:])
                if A:
                    rope(1, "k_ps", "ropek_read")
                if isinstance(i, int) and i == 0:
                    stats(1)
                if C:
                    dve.wait_ge(s["p_ok"], c + 1)
                    dve.wait_ge(s["q_ok"], c + 1)
                    v.tensor_tensor(apq, pq[:, :, 0:D], ea[:, 1, :].rearrange("p (o n) -> p o n", o=1).broadcast_to([P, 2, D]),
                                    ALU.mult).then_inc(s["ap_ok"], 1)
                    dve.wait_ge(s["ap_ok"], c + 1)
                    v.tensor_tensor(apq, apq, ez[:, 2:4, :], ALU.add).then_inc(s["nd_ok"], 1)
                if isinstance(i, int) and i == B + 3:
                    first_rest((3,))
                    top(0, B - 1)
                if Ds and not (isinstance(i, int) and i == B + 1):
                    take_scores(e)
                if Bs:
                    for half in range(2):
                        dve.wait_ge(s["pv_ps"], 4 * t + 2 * half + 2)
                        ov = so[:, half, 0:8 * (HD + 1)].rearrange("p (h d) -> p h d", h=8)
                        v.reciprocal(rinv[:, 8 * half:8 * half + 8], ov[:, :, HD]).then_inc(s["rinv_ok"], 1)
                        dve.wait_ge(s["rinv_ok"], 2 * t + half + 1)
                        wait_prev(dve, s["oT_ps"], t)
                        if isinstance(i, int) and i == 1:
                            dve.wait_ge(s["spare_out"], 32)
                        v.tensor_tensor(o_sb[:, half * D // 2:(half + 1) * D // 2].rearrange("p (h d) -> p h d", h=8),
                                        ov[:, :, 0:HD],
                                        rinv[:, 8 * half:8 * half + 8].rearrange("p (h o) -> p h o", o=1).broadcast_to([P, 8, HD]),
                                        ALU.mult).then_inc(s["o_ok"], 1)
            schedule(dve, body)

            nstep = [0]

            def then(ins):
                nstep[0] += 1
                ins.then_inc(s["step"], 1)
                dve.wait_ge(s["step"], nstep[0])

            top(B - 1, B)
            nstep[0] += B
            dve.wait_ge(s["top_ok"], B)
            v.tensor_tensor(ds12, top8[:, :, 1], top8[:, :, 0], ALU.subtract).then_inc(s["ds_ok"], 1)
            dve.wait_ge(s["step"], nstep[0])
            then(v.tensor_copy(idxf, idx8[:, :, 0:2].rearrange("p b k -> p k b")))
            expert = at["iota"][:, 0:E].rearrange("p (o e) -> p o e", o=1)
            dve.wait_ge(s["const_in"], 16)
            for a in range(2):
                v.tensor_tensor(oh[:, a], expert.broadcast_to([P, B, E]),
                                idxf[:, a].rearrange("p (b o) -> p b o", o=1).broadcast_to([P, B, E]), ALU.is_equal).then_inc(s["oh_ok"], 1)
            dve.wait_ge(s["oh_ok"], 2)
            v.tensor_tensor(picked3, oh[:, 0], oh[:, 1], ALU.add).then_inc(s["oh_ok"], 1)
            dve.wait_ge(s["e12_ok"], 1)
            den, pk = tmp(B), tmp(2, B)
            then(v.tensor_scalar(den, e12, 1.0, None, ALU.add))
            then(v.reciprocal(pk[:, 0], den))
            then(v.tensor_tensor(pk[:, 1], pk[:, 0], e12, ALU.mult))
            pkf = pk.rearrange("p k b -> p (k b)")
            v.tensor_copy(vals[:, :, 0], at["tok"])
            then(v.tensor_copy(phi[:], pkf))
            v.tensor_copy(vals[:, :, 1], phi[:].bitcast(F32))
            then(v.tensor_tensor(vals[:, :, 2], pkf, phi[:].bitcast(F32), ALU.subtract))
            dve.wait_ge(s["rk_ps"], 1)
            tot, cum, cmp, cnt, last, first = tmp(E, B), tmp(E, B), tmp(E, B - 1), tmp(E), tmp(E), tmp(E)
            then(v.tensor_copy(tot, t0[:, P:2 * P].rearrange("p (b e) -> p e b", e=E)))
            then(v.tensor_tensor_scan(cum.rearrange("p e b -> p (e b)"), at["mask"], tot.rearrange("p e b -> p (e b)"),
                                      0.0, ALU.mult, ALU.add))
            then(v.tensor_tensor(cmp, cum[:, :, B - 1:B].broadcast_to([P, E, B - 1]),
                                 at["thr"].rearrange("p (o n) -> p o n", o=1).broadcast_to([P, E, B - 1]), ALU.is_gt))
            then(v.tensor_reduce(cnt, cmp, AX_X, ALU.add))
            then(v.tensor_scalar(cnt, cnt, 1.0, None, ALU.add))
            then(v.tensor_tensor_scan(last, at["ones"][:, 0:E], cnt, 0.0, ALU.mult, ALU.add))
            then(v.tensor_tensor(first, last, cnt, ALU.subtract))
            then(v.tensor_tensor(cum, cum, tot, ALU.subtract))
            then(v.tensor_scalar(first, first, float(P), None, ALU.mult))
            then(v.tensor_tensor(cum, cum, first.rearrange("p (e o) -> p e o", o=1).broadcast_to([P, E, B]), ALU.add))
            sl, pr, row = tmp(B, E), tmp(2, B * E), tmp(2 * B)
            then(v.tensor_tensor(sl, t0[:, 0:P].rearrange("p (b e) -> p b e", e=E), cum.rearrange("p e b -> p b e"), ALU.add))
            then(v.tensor_tensor(pr, oh.rearrange("p a b e -> p a (b e)"),
                                 sl.rearrange("p b e -> p (b e)").rearrange("p (o n) -> p o n", o=1).broadcast_to([P, 2, B * E]), ALU.mult))
            then(v.tensor_reduce(row, pr.rearrange("p a (b e) -> p (a b) e", e=E), AX_X, ALU.add))
            rowi = tmp(2 * B).bitcast(I32)
            divi, modi = tmp(2 * B).bitcast(I32), tmp(2 * B).bitcast(I32)
            modf = tmp(2 * B)
            then(v.tensor_copy(rowi, row))
            v.tensor_scalar(divi, rowi, 7, None, ALU.logical_shift_right)
            then(v.tensor_scalar(modi, rowi, P - 1, None, ALU.bitwise_and))
            v.tensor_copy(divf, divi)
            then(v.tensor_copy(modf, modi))

            def ones(j):
                at_j = slice(j * CH, (j + 1) * CH)
                v.tensor_tensor(one_s[:, at_j], at["iota"][:, 0:NS].rearrange("p (o n) -> p o n", o=1).broadcast_to([P, CH, NS]),
                                divf[:, at_j].rearrange("p (a o) -> p a o", o=1).broadcast_to([P, CH, NS]),
                                ALU.is_equal).then_inc(s["one_ok"], 1)

            def rows(j):
                at_j = slice(j * CH, (j + 1) * CH)
                v.tensor_tensor(sel_p[:, at_j], at["iota"].rearrange("p (o n) -> p o n", o=1).broadcast_to([P, CH, P]),
                                modf[:, at_j].rearrange("p (a o) -> p a o", o=1).broadcast_to([P, CH, P]),
                                ALU.is_equal).then_inc(s["rows_ok"], 1)

            for j in range(NJ):
                ones(j)
                if j > 0:
                    rows(j - 1)
            values(dve, NJ - 1, "last_ok")
            rows(NJ - 1)
            sc, es, prev = tmp(NS, E), tmp(NS), tmp(NS + 1)
            then(v.tensor_tensor(sc, at["iota"][:, 0:NS].rearrange("p (n o) -> p n o", o=1).broadcast_to([P, NS, E]),
                                 last.rearrange("p (o e) -> p o e", o=1).broadcast_to([P, NS, E]), ALU.is_ge))
            then(v.tensor_reduce(es, sc, AX_X, ALU.add))
            v.memset(prev[:, 0:1], 1.0)
            v.memset(prev[:, NS:NS + 1], 1.0)
            then(v.tensor_tensor(prev[:, 1:NS], es[:, 1:NS], es[:, 0:NS - 1], ALU.subtract))
            dve.wait_ge(s["inv_ps"], 1)
            inv3, pad = tmp(3, NS), tmp(NS)
            inv = inv3[:, 0]
            then(v.tensor_copy(inv3, vp[:, 0:3 * NS].rearrange("p (v n) -> p v n", v=3)))
            v.tensor_tensor(w_sb[:], inv3[:, 1], inv3[:, 2], ALU.add)
            then(v.tensor_scalar(pad, inv, 0.0, at["spare"], ALU.is_equal, ALU.mult))
            v.memset(ids_sb[:, NS:NS + 1], 0)
            then(v.scalar_tensor_tensor(out=ids_sb[:, 0:NS], in0=inv, scalar=-1.0, in1=pad, op0=ALU.add, op1=ALU.add))
            v.tensor_copy(idg[:], ids_sb[:, 0:1]).then_inc(s["m_idg"], 1)
            half2, more, odd, own = tmp(NS), tmp(NS), tmp(NS), tmp(NS)
            v.tensor_copy(tab[:, 0, :], es)
            v.memset(half2[:, 0:1], 0.0)
            then(v.tensor_tensor(half2[:, 1:NS], prev[:, 0:NS - 1], prev[:, 1:NS], ALU.is_gt))
            then(v.tensor_tensor(more, prev[:, 0:NS], prev[:, 1:NS + 1], ALU.mult))
            then(v.tensor_tensor(half2, half2, more, ALU.add))
            then(v.scalar_tensor_tensor(out=half2, in0=half2, scalar=2.0, in1=prev[:, 0:NS], op0=ALU.mult, op1=ALU.add))
            then(v.scalar_tensor_tensor(out=half2, in0=es, scalar=E - 1.0, in1=half2, op0=ALU.is_lt, op1=ALU.mult))
            then(v.tensor_scalar(tab[:, 1, :], tab[:, 0, :], 1, None, ALU.bitwise_and))
            then(v.tensor_copy(odd, tab[:, 1, :]))
            then(v.scalar_tensor_tensor(out=own, in0=es, scalar=8.0, in1=half2, op0=ALU.mult, op1=ALU.add))
            then(v.tensor_scalar(own, own, 12.0, None, ALU.add))
            then(v.scalar_tensor_tensor(out=tab[:, 1, :], in0=odd, scalar=-4.0, in1=own, op0=ALU.mult, op1=ALU.add))
            v.tensor_scalar(tab[:, 0, 0:1], es[:, 0:1], 2.0, 2.0, ALU.mult, ALU.add)
            then(v.tensor_scalar(own, es, 2.0, 2.0, ALU.mult, ALU.add))
            then(v.tensor_tensor(tab[:, 0, 1:NS], odd[:, 0:NS - 1], own[:, 1:NS], ALU.add))
            v.tensor_scalar(nslot[:, 0:1], last[:, E - 1:E], -3.0, None, ALU.add)
            v.memset(hold[:], 0.0).then_inc(s["tab_set"], 1)
            dve.wait_ge(s["tab_set"], 1)
            dve.wait_ge(s["m_xg"], 16)
            v.tensor_copy(idg[:], ids_sb[:, 1:2]).then_inc(s["m_idg"], 1)

            def moe(k, X, M1, M2):
                if M2:
                    dve.wait_ge(s["m_hhi"], k - 1)
                    v.tensor_tensor(oT_lo[:, 0:KF, :].rearrange("p k n -> p (k n)"), vp[:, 0:KF * P],
                                    oT_hi[:, 0:KF, :].rearrange("p k n -> p (k n)").bitcast(F32), ALU.subtract).then_inc(s["m_hlo"], 1)
                    split_next(nc.vector, k)
                if M1:
                    dve.wait_ge(s["m_silu"], k)
                    wait_prev(dve, s["m_hT"], k - 1)
                    v.tensor_tensor(hsb[:, 0:FH], qk_ps[:, 1, 0:FH], gsb, ALU.mult).then_inc(s["m_h"], 1)
                if X:
                    dve.wait_ge(s["m_xhi"], k + 1)
                    v.tensor_tensor(xnT_lo[:].rearrange("p k n -> p (k n)"), t0[:],
                                    xnT_hi[:].rearrange("p k n -> p (k n)").bitcast(F32), ALU.subtract).then_inc(s["m_xlo"], 1)
                    dve.wait_ge(s["m_xg"], 16 * (k + 2))
                    v.tensor_scalar(idg[:], ids_sb[:, bass.ds(k + 2, 1)], 0.0, None, ALU.add).then_inc(s["m_idg"], 1)
                if M2:
                    dve.wait_ge(s["m_y"], k - 1)
                    wait_prev(dve, s["m_sc"], 16 * (k - 2))
                    v.tensor_scalar(ids_out[:], ids_sb[:, bass.ds(k - 2, 1)], 0.0, None, ALU.add)
                    v.tensor_scalar(o_sb[:], tp[:, 0, :], w_sb[:, bass.ds(k - 2, 1)], None, ALU.mult).then_inc(s["m_yok"], 1)
            slots(dve, moe)


def kernel(**inputs):
    import numpy as np
    import concourse.bacc as bacc
    from concourse.bass_utils import run_bass_kernel_spmd

    f32 = np.float32
    T, DM, HW = 128, 512, 32
    a = {n: np.ascontiguousarray(v) for n, v in inputs.items()}
    NB = a["x"].shape[0]
    freqs = (1.0 / f32(10000.0) ** (np.arange(0, HW, 2, dtype=f32) / f32(HW))).astype(f32)
    angle = np.outer(np.arange(T, dtype=f32), freqs).astype(f32)
    sin = np.repeat(np.sin(angle), 2, axis=-1)
    sin[:, 0::2] *= -1
    NE, FF, KB = a["L0_ffn_W1"].shape[0], a["L0_ffn_W1"].shape[1], DM // 128
    moe = np.zeros((NE, 128, 2 * KB * FF + 3 * DM), f32)
    w12 = moe[:, :, :2 * KB * FF].reshape(NE, 128, KB, 2, FF)
    for g, n in enumerate(("L0_ffn_W1", "L0_ffn_W2")):
        w12[:, :, :, g, :] = a[n].reshape(NE, FF, KB, 128).transpose(0, 3, 2, 1)
    w3 = moe[:, :, 2 * KB * FF:].reshape(NE, 128, 3, DM)
    for k in range(3):
        n = min(128, FF - 128 * k)
        w3[:, :n, k, :] = a["L0_ffn_W3"][:, :, 128 * k:128 * k + n].transpose(0, 2, 1)
    row = np.arange(128)
    col = lambda v: np.broadcast_to(np.asarray(v, f32), (128, len(v)))
    consts = {
        "ident": np.eye(128), "cos": np.repeat(np.cos(angle), 2, axis=-1), "sin": sin, "iota": col(row),
        "tri": np.triu(np.ones((128, 128)), 1), "ones": np.ones((128, 128)),
        "mask": col(np.tile(np.arange(NB) > 0, NE)), "thr": col(128 * np.arange(1, NB)),
        "tok": row[:, None] + 1 + 128 * np.tile(np.arange(NB), 2)[None, :], "spare": NB * T + 1 + row[:, None],
    }
    arrays = {
        "x": a["x"].reshape(NB * T, DM),
        "ctxT": np.ascontiguousarray(a["ctx_2048"].reshape(NB, T, KB, 128).transpose(0, 3, 2, 1)),
        "w_qkv": a["L0_attn_w_qkv"], "w_proj": a["L0_attn_w_proj"],
        "wkv_wu": np.ascontiguousarray(np.stack([a["L0_xattn_w"], a["L0_xattn_u"]]).reshape(2, KB, 128).transpose(2, 0, 1)),
        "wgT": np.ascontiguousarray(a["L0_ffn_Wg"].reshape(NE, KB, 128).transpose(2, 1, 0)),
        "w_moe": moe,
        "consts": np.concatenate([consts[n].astype(f32) for n, _ in CONSTS], axis=1),
    }
    nc = bacc.Bacc("TRN2", target_bir_lowering=False, num_devices=1)
    args = [nc.dram_tensor(n, v.shape, mybir.dt.from_np(v.dtype), kind="ExternalInput").ap() for n, v in arrays.items()]
    x3 = nc.dram_tensor("x3n_rows", (NB * T + 128, DM), F32).ap()
    out = nc.dram_tensor("y_out", (NB * T + 128, DM), F32, kind="ExternalOutput").ap()
    decoder(nc, *args, x3, out)
    r = run_bass_kernel_spmd(nc, [arrays], core_ids=[0])
    return r.results[0]["y_out"][:NB * T].reshape(NB, T, DM)
```
